# Optimizing a Trainium2 kernel written in Bass

```python
import numpy as np
import jax
import jax.numpy as jnp

def _softmax(x, axis=-1):
    return jax.nn.softmax(x, axis=axis)

def _gelu(x):
    return jax.nn.gelu(x, approximate=True)

def _silu(x):
    return jax.nn.silu(x)

def _sigmoid(x):
    return jax.nn.sigmoid(x)

def _layernorm(x, axis=-1, eps=1e-05):
    m = jnp.mean(x, axis=axis, keepdims=True)
    v = jnp.var(x, axis=axis, keepdims=True)
    return (x - m) / jnp.sqrt(v + eps)

def _scatter_add(tgt, idx, src, axis=0):
    return tgt.at[idx].add(src)

def _segment_sum(src, seg, n):
    return jax.ops.segment_sum(src, seg, n)
kernel_name = 'mk_hybrid_d1_jaxref_r8_07c625'

def setup_inputs(seed: int=0):
    np.random.seed(seed)
    _w = jnp.asarray

    def _L0_attn_a_setup():
        import jax, jax.numpy as jnp
        import numpy as np
        B, M, D = (8, 256, 128)

        def _rope_tables(m, d):
            i = jnp.arange(d // 2, dtype=jnp.float32)
            theta = jnp.power(jnp.float32(10000.0), -2.0 * (i - 1.0) / d)
            ang = jnp.arange(m, dtype=jnp.float32)[:, None] * theta[None, :]
            return (jnp.cos(ang), jnp.sin(ang))

        def _rotate(t, cos, sin):
            te, to = (t[..., 0::2], t[..., 1::2])
            re = te * cos + to * sin
            ro = -te * sin + to * cos
            return jnp.stack([re, ro], axis=-1).reshape(t.shape)
        key = jax.random.key(seed)
        kx, kq, kk, kv = jax.random.split(key, 4)
        x = jax.random.normal(kx, (B, M, D), dtype=jnp.float32)
        wq = jax.random.normal(kq, (D, D), dtype=jnp.float32) * 0.02
        wk = jax.random.normal(kk, (D, D), dtype=jnp.float32) * 0.02
        wv = jax.random.normal(kv, (D, D), dtype=jnp.float32) * 0.02
        return {'x': x, 'wq': wq, 'wk': wk, 'wv': wv}
    _L0_attn_a_in = _L0_attn_a_setup()

    def _L0_attn_b_setup():
        import jax, jax.numpy as jnp
        import numpy as np
        import math
        B, T, C = (2, 256, 128)
        H, DK, DV = (16, 64, 64)
        key = jax.random.key(seed)
        ks = jax.random.split(key, 5)
        x = jax.random.normal(ks[0], (B, T, C), dtype=jnp.float32)
        w_q = jax.random.normal(ks[1], (H, DK, C), dtype=jnp.float32) / math.sqrt(C)
        w_k = jax.random.normal(ks[2], (H, DK, C), dtype=jnp.float32) / math.sqrt(C)
        w_v = jax.random.normal(ks[3], (H, DV, C), dtype=jnp.float32) / math.sqrt(C)
        w_o = jax.random.normal(ks[4], (H * DV, C), dtype=jnp.float32) / math.sqrt(C)
        return {'x': x, 'w_q': w_q, 'w_k': w_k, 'w_v': w_v, 'w_o': w_o}
    _L0_attn_b_in = _L0_attn_b_setup()

    def _L0_ffn_setup():
        import jax, jax.numpy as jnp
        import numpy as np
        B, S, D, F, E = (4, 256, 128, 512, 8)
        key = jax.random.key(seed)
        ks = jax.random.split(key, 7)
        s1 = 1.0 / np.sqrt(D)
        s2 = 1.0 / np.sqrt(F)
        x = jax.random.normal(ks[0], (B, S, D), dtype=jnp.float32)
        W1 = jax.random.uniform(ks[1], (E, D, F), jnp.float32, -s1, s1)
        b1 = jax.random.uniform(ks[2], (E, F), jnp.float32, -s1, s1)
        W2 = jax.random.uniform(ks[3], (E, F, D), jnp.float32, -s2, s2)
        b2 = jax.random.uniform(ks[4], (E, D), jnp.float32, -s2, s2)
        Wr = jax.random.uniform(ks[5], (D, E), jnp.float32, -s1, s1)
        br = jax.random.uniform(ks[6], (E,), jnp.float32, -s1, s1)
        return {'x': x, 'W1': W1, 'b1': b1, 'W2': W2, 'b2': b2, 'Wr': Wr, 'br': br}
    _L0_ffn_in = _L0_ffn_setup()
    _d = {'L0_attn_a_x': _L0_attn_a_in['x'], 'L0_attn_a_wq': _L0_attn_a_in['wq'], 'L0_attn_a_wk': _L0_attn_a_in['wk'], 'L0_attn_a_wv': _L0_attn_a_in['wv'], 'L0_attn_b_w_q': _L0_attn_b_in['w_q'], 'L0_attn_b_w_k': _L0_attn_b_in['w_k'], 'L0_attn_b_w_v': _L0_attn_b_in['w_v'], 'L0_attn_b_w_o': _L0_attn_b_in['w_o'], 'L0_ffn_W1': _L0_ffn_in['W1'], 'L0_ffn_b1': _L0_ffn_in['b1'], 'L0_ffn_W2': _L0_ffn_in['W2'], 'L0_ffn_b2': _L0_ffn_in['b2'], 'L0_ffn_Wr': _L0_ffn_in['Wr'], 'L0_ffn_br': _L0_ffn_in['br']}
    _x0 = _d['L0_attn_a_x']
    _d['L0_attn_a_x'] = jax.random.normal(jax.random.fold_in(jax.random.key(seed), 1), (16, 256, 128), dtype=_x0.dtype)
    del _x0
    return _d

def reference(L0_attn_a_x, L0_attn_a_wq, L0_attn_a_wk, L0_attn_a_wv, L0_attn_b_w_q, L0_attn_b_w_k, L0_attn_b_w_v, L0_attn_b_w_o, L0_ffn_W1, L0_ffn_b1, L0_ffn_W2, L0_ffn_b2, L0_ffn_Wr, L0_ffn_br):

    def _L0_attn_a_ref(x, wq, wk, wv):
        import jax, jax.numpy as jnp
        import numpy as np
        B, M, D = (8, 256, 128)

        def _rope_tables(m, d):
            i = jnp.arange(d // 2, dtype=jnp.float32)
            theta = jnp.power(jnp.float32(10000.0), -2.0 * (i - 1.0) / d)
            ang = jnp.arange(m, dtype=jnp.float32)[:, None] * theta[None, :]
            return (jnp.cos(ang), jnp.sin(ang))

        def _rotate(t, cos, sin):
            te, to = (t[..., 0::2], t[..., 1::2])
            re = te * cos + to * sin
            ro = -te * sin + to * cos
            return jnp.stack([re, ro], axis=-1).reshape(t.shape)
        b, m, d = x.shape
        q = x @ wq.T
        k = x @ wk.T
        v = x @ wv.T
        cos, sin = _rope_tables(m, d)
        qr = _rotate(q, cos, sin)
        kr = _rotate(k, cos, sin)
        scale = 1.0 / jnp.sqrt(jnp.float32(d))
        scores = jnp.einsum('bqd,bkd->bqk', qr, kr) * scale
        attn = jax.nn.softmax(scores, axis=-1)
        return jnp.einsum('bqk,bkd->bqd', attn, v)

    def _L0_attn_b_ref(x, w_q, w_k, w_v, w_o):
        import jax, jax.numpy as jnp
        import numpy as np
        import math
        B, T, C = (2, 256, 128)
        H, DK, DV = (16, 64, 64)
        dk = w_q.shape[1]
        q = jnp.einsum('ntc,hdc->nhtd', x, w_q)
        k = jnp.einsum('ntc,hdc->nhtd', x, w_k)
        v = jnp.einsum('ntc,hdc->nhtd', x, w_v)
        a = jnp.einsum('nhtd,nhsd->nhts', q, k) / jnp.sqrt(jnp.asarray(dk, x.dtype))
        t = a.shape[-1]
        mask = jnp.arange(t)[:, None] < jnp.arange(t)[None, :]
        a = jnp.where(mask[None, None], jnp.asarray(-jnp.inf, a.dtype), a)
        a = jax.nn.softmax(a, axis=-1)
        y = jnp.einsum('nhts,nhsd->nthd', a, v)
        y = y.reshape(y.shape[0], y.shape[1], -1)
        return y @ w_o

    def _L0_ffn_ref(x, W1, b1, W2, b2, Wr, br):
        import jax, jax.numpy as jnp
        import numpy as np
        B, S, D, F, E = (4, 256, 128, 512, 8)
        b, s, d = x.shape
        e = Wr.shape[1]
        logits = x @ Wr + br
        idx = jnp.argmax(logits, axis=-1)
        probs = jax.nn.softmax(logits, axis=-1)
        gates = jnp.take_along_axis(probs, idx[..., None], axis=-1)[..., 0]
        xf = x.reshape(-1, d)
        idxf = idx.reshape(-1)
        gf = gates.reshape(-1)
        out = jnp.zeros_like(xf)
        for ei in range(e):
            h = jax.nn.gelu(xf @ W1[ei] + b1[ei], approximate=False)
            y = h @ W2[ei] + b2[ei]
            mask = (idxf == ei).astype(xf.dtype)
            out = out + y * (gf * mask)[:, None]
        return out.reshape(b, s, d)
    x = L0_attn_a_x
    x = x + _L0_attn_a_ref(_layernorm(x, axis=-1), L0_attn_a_wq, L0_attn_a_wk, L0_attn_a_wv)
    x = x + _L0_ffn_ref(_layernorm(x, axis=-1), L0_ffn_W1, L0_ffn_b1, L0_ffn_W2, L0_ffn_b2, L0_ffn_Wr, L0_ffn_br)
    x = x + _L0_attn_b_ref(_layernorm(x, axis=-1), L0_attn_b_w_q, L0_attn_b_w_k, L0_attn_b_w_v, L0_attn_b_w_o)
    x = x + _L0_ffn_ref(_layernorm(x, axis=-1), L0_ffn_W1, L0_ffn_b1, L0_ffn_W2, L0_ffn_b2, L0_ffn_Wr, L0_ffn_br)
    return x

_drawn_inputs = setup_inputs


def setup_inputs(seed=0):
    import zlib

    import numpy as np

    out = dict(_drawn_inputs(seed))
    spreads = {}
    factors = {'L0_attn_a_wq': 8.0, 'L0_attn_a_wk': 8.0, 'L0_ffn_b1': 5.938, 'L0_ffn_b2': 4.257}
    for name, (base, spread) in spreads.items():
        noise = np.random.default_rng([zlib.crc32(name.encode()), seed]).standard_normal(out[name].shape)
        drawn = base * np.exp(spread * noise) if base else spread * noise
        out[name] = jnp.asarray(drawn.astype(out[name].dtype))
    for name, factor in factors.items():
        out[name] = (out[name] * factor).astype(out[name].dtype)
    return out
```

```python
from contextlib import ExitStack

import numpy as np
import concourse.bass as bass
from concourse import mybir

F32 = mybir.dt.float32
BF16 = mybir.dt.bfloat16
I32 = mybir.dt.int32
ALU = mybir.AluOpType
ACT = mybir.ActivationFunctionType
AX = mybir.AxisListType

P = 128
NB, M, D = 16, 256, 128
TPB = M // P
NT = NB * TPB
H, DK = 16, 64
NPAIR = H // 2
E, F = 8, 512
FC = F // P
GROUPS = 2
GB = NB // GROUPS
GT = GB * TPB
NJ = GT + E - 1
W1W = F + FC
EPS = 1e-5
SCALE_A = float(1.0 / np.sqrt(np.float32(D)))
SCALE_B = float(1.0 / np.sqrt(np.float32(DK)))
MASKED = -3.0e38
YCHUNKS = ((0, 6), (6, 12), (12, 18), (18, NJ))
XCHUNKS = ((0, 4), (4, NJ))

C_ID, C_UP, C_ONE, C_MASK = 0, P, 2 * P, 3 * P
C_E8 = 4 * P
C_SCAN = C_E8 + E
C_TILE = C_SCAN + E * GT
C_W = C_TILE + NJ * E


def ds(i, n=1):
    return bass.ds(i, n)


def fixed(v):
    return isinstance(v, int)


def wait(eng, sem, value):
    if not fixed(value) or value > 0:
        eng.wait_ge(sem, value)


def turns(eng, body, first, last):
    with eng.Fori(first // 2, last // 2) as turn:
        for u in range(2):
            body(turn * 2 + u, u)


def peeled(body, first, last):
    for s in range(first, last):
        body(s, s % 2)


def has(b, n=NB):
    return not fixed(b) or 0 <= b < n


def build(nc, x, wqk_a, wv_a, rope, w_q, w_k, wv_b, w_o, W1, b1t, W2, b2, Wr, br, cst, out):
    ctx = ExitStack()
    with ctx:
        def sb(name, shape, dt=F32):
            return ctx.enter_context(nc.sbuf_tensor(name, shape, dt))

        def sem(name):
            return ctx.enter_context(nc.semaphore(name))

        xs_dram = [nc.dram_tensor(f"xs_dram{g}", [P * NJ, D], F32, kind="Internal").ap() for g in range(GROUPS)]
        ys_dram = [nc.dram_tensor(f"ys_dram{g}", [P * NJ, D], F32, kind="Internal").ap() for g in range(GROUPS)]

        X = sb("X", [P, NT, D])
        CST = sb("CST", [P, C_W])
        ident = CST[:, C_ID:C_ID + P]
        identb = sb("identb", [P, P], BF16)
        upperb = sb("upperb", [P, P], BF16)
        onesb = sb("onesb", [P, P], BF16)
        maskb = sb("maskb", [P, P], BF16)
        half = sb("half", [P, TPB])
        WQK = sb("WQK", [P, 4, D])
        WVA = sb("WVA", [P, D])
        ROPE = sb("ROPE", [P, 2, 2 * M])
        QK = sb("QK", [P, H, D])
        WVB = sb("WVB", [P, H * DK])
        WO = sb("WO", [P, NPAIR, D])
        W1S = sb("W1S", [P, E, W1W])
        W2S = sb("W2S", [P, E, FC, D])
        B2S = sb("B2S", [P, E, D])
        WRS = sb("WRS", [P, E])
        BRS = sb("BRS", [P, E])
        LN = {}
        for n in "AFB":
            LN[n] = {
                "stats": sb(f"stats{n}", [P, 2, TPB, 6]), "mv": sb(f"mv{n}", [P, 2, TPB, 2]),
                "var": sb(f"var{n}", [P, 2, TPB]), "rstd": sb(f"rstd{n}", [P, 2, TPB]),
                "out": sb(f"ln{n}", [P, 2, TPB, D]),
                "s_stats": sem(f"ln{n}_stats"), "s_mv": sem(f"ln{n}_mv"), "s_var": sem(f"ln{n}_var"),
                "s_rstd": sem(f"ln{n}_rstd"), "s_out": sem(f"ln{n}_out"),
            }
        xnT = sb("xnT", [P, 2, M])
        rot = sb("rot", [P, 2, 2 * M])
        qk = sb("qk", [P, 2, 2, M])
        va = sb("va", [P, 2, TPB, D])
        mxa, nba, rsa, ria = (sb(n, [P, 2, TPB]) for n in ("mxa", "nba", "rsa", "ria"))
        pa = sb("pa", [P, 2, TPB, M])
        pTa = sb("pTa", [P, 2, TPB, M])
        gT = sb("gT", [P, 2, M])
        mxb, nbb, rsb, rib = (sb(n, [P, 4, TPB]) for n in ("mxb", "nbb", "rsb", "rib"))
        pb = sb("pb", [P, 4, 3 * P])
        pTb = sb("pTb", [P, 2, 3 * P])
        vb = sb("vb", [P, 2, TPB, H * DK])
        yT = sb("yT", [P, 2, NPAIR, M])
        WQB = yT[0:DK, 0, :, :].rearrange("p a (c d) -> p (a c) d", c=2)
        WKB = yT[0:DK, 1, :, :].rearrange("p a (c d) -> p (a c) d", c=2)
        TOK = sb("TOK", [P, NT, D])
        fT = sb("fT", [P, 2, M])
        LG = sb("LG", [P, NT, E])
        GATE = sb("GATE", [P, NT])
        POS = sb("POS", [P, NT], I32)
        TE = sb("TE", [P, GROUPS, NJ], I32)
        r_mx = sb("r_mx", [P, GT])
        r_sh = sb("r_sh", [P, GT, E])
        r_ex = sb("r_ex", [P, GT, E])
        r_den = sb("r_den", [P, GT])
        r_eq = sb("r_eq", [P, GT, E])
        r_best = sb("r_best", [P, GT])
        r_ps = sb("r_ps", [P, 2 * E * GT])
        r_hot = sb("r_hot", [P, E, GT], BF16)
        r_inc = sb("r_inc", [P, E, GT])
        r_exc = sb("r_exc", [P, E, GT])
        r_cnt = sb("r_cnt", [P, E], I32)
        r_cnts = sb("r_cnts", [P, E], I32)
        r_nt = sb("r_nt", [P, E])
        r_cum = sb("r_cum", [P, E])
        r_base = sb("r_base", [P, E])
        r_pos = sb("r_pos", [P, GT])
        r_posi = sb("r_posi", [P, GT], I32)
        r_tile = sb("r_tile", [P, GT], I32)
        r_tilef = sb("r_tilef", [P, GT])
        r_cmp = sb("r_cmp", [P, NJ, E])
        r_te = sb("r_te", [P, NJ])
        XY = sb("XY", [P, GROUPS, NJ, D])
        xs1 = sb("xs1", [P, 2, D])
        w1b1 = sb("w1b1", [P, 2, W1W])
        xsT = sb("xsT", [P, 2, P])
        hT = sb("hT", [P, 2, FC, P])
        PS = ctx.enter_context(nc.psum_tensor("PS", [P, 8, 512], F32))

        s_cst, s_x0, s_x1, s_wa, s_wb, s_wr, s_w1, s_w2, s_xs0 = (
            sem(n) for n in ("cst_in", "x_first_in", "x_rest_in", "w_attn_a_in", "w_attn_b_in", "w_router_in",
                             "w1_in", "w2_in", "xs_zeroed"))
        s_castb, s_zero = sem("consts_cast"), sem("zeros_set")
        (a_xT_ps, a_xT, a_qk_ps, a_rot, a_rope, a_v_ps, a_v, a_scores, a_max, a_nb, a_exp, a_rinv, a_pT_ps, a_pT,
         a_out_ps, a_x) = (sem("a_" + n) for n in (
             "xT_ps", "xT", "qk_ps", "rot", "rope", "v_ps", "v", "scores", "max", "nb", "exp", "rinv", "pT_ps", "pT",
             "out_ps", "x"))
        r_xT_ps, r_xT, r_tok, r_lg_ps, r_lg = (sem("r_" + n) for n in ("xT_ps", "xT", "tok", "lg_ps", "lg"))
        r_step, r_exp, r_pre_ps = (sem("r_" + n) for n in ("step", "exp", "pre_ps"))
        scattered = [sem(f"scattered{k}") for k in range(4)]
        gathered = [sem(f"gathered{k}") for k in range(4)]
        xs_in = [[sem(f"xs_in{k}_{c}") for c in range(len(XCHUNKS))] for k in range(4)]
        ys_out = [sem(f"ys_out{k}") for k in range(4)]
        f_in, f_xT_ps, f_xT, f_w1, f_h_ps, f_gelu, f_y_ps, f_y = (
            sem("f_" + n) for n in ("in", "xT_ps", "xT", "w1", "h_ps", "gelu", "y_ps", "y"))
        b_qk_ps, b_qk = sem("b_qk_ps"), sem("b_qk")
        b_comb, b_xT_ps, b_xT, b_v_ps, b_v, b_out_ps, b_x = (
            sem("b_" + n) for n in ("comb", "xT_ps", "xT", "v_ps", "v", "out_ps", "x"))
        b_g_ps, b_g, b_s_ps, b_max, b_nb, b_exp, b_rinv, b_p, b_pT_ps, b_pT, b_av, b_y = (
            sem("b_h" + n) for n in ("g_ps", "g", "s_ps", "max", "nb", "exp", "rinv", "p", "pT_ps", "pT", "av", "y"))
        dve_waited, pool_waited = sem("dve_waited"), sem("pool_waited")
        x_done, s_out = sem("x_done"), sem("out_stored")

        block = ctx.enter_context(nc.Block())

        @block.sync
        def _(sp):
            xv = x.rearrange("b (t p) d -> p (b t) d", p=P)
            sp.dma_start(CST[:, :], cst).then_inc(s_cst, 16)
            sp.dma_start(X[:, 0:4, :], xv[:, 0:4, :]).then_inc(s_x0, 16)
            sp.dma_start(WQK[:, :, :], wqk_a).then_inc(s_wa, 16)
            sp.dma_start(ROPE[:, :, :], rope).then_inc(s_wa, 16)
            sp.dma_start(WVA[:, :], wv_a).then_inc(s_wa, 16)
            sp.dma_start(WRS[:, :], Wr).then_inc(s_wr, 16)
            sp.dma_start(BRS[:, :], br.rearrange("(a e) -> a e", a=1).to_broadcast([P, E])).then_inc(s_wr, 16)
            sp.dma_start(X[:, 4:NT, :], xv[:, 4:NT, :]).then_inc(s_x1, 16)
            sp.wait_ge(s_zero, 1)
            for g in range(GROUPS):
                sp.dma_start(xs_dram[g].rearrange("(p j) d -> p j d", p=P), XY[:, g, :, :]).then_inc(s_xs0, 16)
            sp.dma_start(W1S[:, :, 0:F], W1.rearrange("e d f -> d e f")).then_inc(s_w1, 16)
            sp.dma_start(W1S[:, :, F:W1W], b1t).then_inc(s_w1, 16)
            sp.dma_start(W2S[:, :, :, :], W2.rearrange("e (c p) d -> p e c d", p=P)).then_inc(s_w2, 16)
            sp.dma_start(B2S[:, :, :].rearrange("p e d -> p (e d)"),
                         b2.rearrange("(a e) d -> a (e d)", a=1).to_broadcast([P, E * D])).then_inc(s_w2, 16)
            sp.dma_start(WQB, w_q.rearrange("h k c -> k h c")).then_inc(s_wb, 16)
            sp.dma_start(WKB, w_k.rearrange("h k c -> k h c")).then_inc(s_wb, 16)
            sp.dma_start(WVB[:, :], wv_b).then_inc(s_wb, 16)
            sp.dma_start(WO[:, :, :], w_o.rearrange("(a p) d -> p a d", p=P)).then_inc(s_wb, 16)
            for k in range(4):
                g = k % GROUPS
                xsv = xs_dram[g].rearrange("(p j) d -> p j d", p=P)
                ysv = ys_dram[g].rearrange("(p j) d -> p j d", p=P)
                sp.wait_ge(scattered[k], 16 * GT)
                if k >= GROUPS:
                    sp.wait_ge(gathered[k - GROUPS], 16 * GT)
                for c, (j0, j1) in enumerate(XCHUNKS):
                    sp.dma_start(XY[:, g, j0:j1, :], xsv[:, j0:j1, :]).then_inc(xs_in[k][c], 16)
                if k % 2 == 1:
                    for kk in (k - 1, k):
                        gg = kk % GROUPS
                        yv = ys_dram[gg].rearrange("(p j) d -> p j d", p=P)
                        for j0, j1 in YCHUNKS:
                            sp.wait_ge(f_y, NJ * kk + j1)
                            sp.dma_start(yv[:, j0:j1, :], XY[:, gg, j0:j1, :]).then_inc(ys_out[kk], 16)
            ov = out.rearrange("b (t p) d -> p (b t) d", p=P)
            for c in range(4):
                sp.wait_ge(x_done, c + 1)
                sp.dma_start(ov[:, 8 * c:8 * c + 8, :], X[:, 8 * c:8 * c + 8, :]).then_inc(s_out, 16)
            sp.wait_ge(s_out, 64)

        @block.gpsimd
        def _(pool):
            nc.gpsimd.memset(XY[:, :, :, :], 0.0).then_inc(s_zero, 1)
            pool.wait_ge(s_castb, 1)

            def rstd(ln, n, slot):
                pool.wait_ge(ln["s_var"], n + 1)
                nc.gpsimd.tensor_tensor(ln["rstd"][:, slot, :], ln["var"][:, slot, :], half[:, :],
                                        ALU.pow).then_inc(ln["s_rstd"], 1)

            def scatter(k, t):
                tile = GT * (k % GROUPS) + t
                nc.gpsimd.indirect_dma_start(
                    out=xs_dram[k % GROUPS], out_offset=bass.IndirectOffsetOnAxis(ap=POS[:, tile:tile + 1], axis=0),
                    in_=TOK[:, tile, :], in_offset=None).then_inc(scattered[k], 16)

            def before_scatters(k):
                pool.wait_ge(r_step, STEPS * (k + 1))
                pool.wait_ge(r_tok, GB * (k + 1))
                if k < GROUPS:
                    pool.wait_ge(s_xs0, 32)
                else:
                    for c in range(len(XCHUNKS)):
                        pool.wait_ge(xs_in[k - GROUPS][c], 16)

            def gather(k, t):
                tile = GT * (k % GROUPS) + t
                nc.gpsimd.indirect_dma_start(
                    out=TOK[:, tile, :], out_offset=None, in_=ys_dram[k % GROUPS],
                    in_offset=bass.IndirectOffsetOnAxis(ap=POS[:, tile:tile + 1], axis=0)).then_inc(gathered[k], 16)

            def attn_a(s, u):
                if has(s):
                    rstd(LN["A"], s, u)
                if has(s - 4):
                    rstd(LN["F"], s - 4, u)

            peeled(attn_a, 0, 8)
            turns(pool, attn_a, 8, 14)
            for s in range(14, NB + 5):
                attn_a(s, s % 2)
                if s == 14:
                    before_scatters(0)
                for t in range(3 * (s - 14), min(3 * (s - 13), GT)):
                    scatter(0, t)
            before_scatters(1)
            for t in range(GT):
                scatter(1, t)
            pool.wait_ge(ys_out[0], 16 * len(YCHUNKS))
            for t in range(GT):
                gather(0, t)

            def attn_b(s, u, more=None):
                hb, fb = s - 1, s - 2
                for h in range(H):
                    b, hh = (hb, h - 2) if h >= 2 else (fb, h - 2 + H)
                    if has(b):
                        pool.wait_ge(b_rinv, b * H + (hh + 1))
                        pool.sem_inc(pool_waited)
                        nc.gpsimd.tensor_scalar(pb[:, hh % 4, 0:P], pb[:, hh % 4, 0:P], rib[:, hh % 4, 0:1], 1.0,
                                                ALU.mult, ALU.mult)
                        nc.gpsimd.tensor_scalar(pb[:, hh % 4, P:3 * P], pb[:, hh % 4, P:3 * P], rib[:, hh % 4, 1:2],
                                                1.0, ALU.mult, ALU.mult).then_inc(b_p, 1)
                    if h == 8 and has(fb):
                        rstd(LN["F"], fb + NB, u)
                    if h == 10 and has(s):
                        rstd(LN["B"], s, u)
                    if more is not None:
                        more(h)

            def gather1(h):
                if h == 0:
                    pool.wait_ge(ys_out[1], 16 * len(YCHUNKS))
                gather(1, h)

            def scatter2(h):
                if h == 0:
                    before_scatters(2)
                scatter(2, h)

            attn_b(0, 0)
            attn_b(1, 1, gather1)
            peeled(attn_b, 2, 4)
            turns(pool, attn_b, 4, 10)
            attn_b(10, 0)
            attn_b(11, 1, scatter2)
            turns(pool, attn_b, 12, 16)
            peeled(attn_b, 16, 18)
            before_scatters(3)
            for t in range(GT):
                scatter(3, t)
            for k in (2, 3):
                pool.wait_ge(ys_out[k], 16 * len(YCHUNKS))
                for t in range(GT):
                    gather(k, t)

        @block.scalar
        def _(act):
            def router_copies(n, tile, slot, bank):
                act.wait_ge(LN["F"]["s_out"], n + 1)
                nc.scalar.copy(TOK[:, ds(tile, TPB), :], LN["F"]["out"][:, slot, :, :]).then_inc(r_tok, 1)
                act.wait_ge(r_xT_ps, n + 1)
                wait(act, r_lg_ps, n - 1)
                nc.scalar.copy(fT[:, slot, :], PS[:, bank, 0:M]).then_inc(r_xT, 1)

            def attn_a(s, u):
                v = (u + 1) % 2
                b = s - 1
                if has(b):
                    act.wait_ge(a_xT_ps, b + 1)
                    wait(act, a_v_ps, b - 1)
                    nc.scalar.copy(xnT[:, v, :], PS[:, 4, 0:M]).then_inc(a_xT, 1)
                b = s - 3
                if has(b):
                    act.wait_ge(a_pT_ps, b + 1)
                    wait(act, a_out_ps, b - 1)
                    nc.scalar.copy(pTa[:, v, :, :], PS[:, 3, :].rearrange("p (t m) -> p t m", t=TPB)).then_inc(a_pT, 1)
                b = s - 2
                if has(b):
                    act.wait_ge(a_nb, b + 1)
                    wait(act, a_pT_ps, b - 1)
                    wait(act, a_rinv, b - 1)
                    for i in range(TPB):
                        last = nc.scalar.activation(pa[:, u, i, :], PS[:, 2, i * M:(i + 1) * M], ACT.Exp,
                                                    bias=nba[:, u, i:i + 1], scale=SCALE_A,
                                                    accum_out=rsa[:, u, i:i + 1])
                    last.then_inc(a_exp, 1)
                b = s - 1
                if has(b):
                    act.wait_ge(a_v_ps, b + 1)
                    wait(act, a_out_ps, b - 1)
                    nc.scalar.copy(va[:, v, :, :], PS[:, 5, 0:TPB * D].rearrange("p (t d) -> p t d", t=TPB)).then_inc(a_v, 1)
                b = s - 5
                if has(b):
                    router_copies(b, TPB * b, v, 7)

            def route(k):
                act.wait_ge(r_step, STEPS * k + SHIFT_STEP)
                nc.scalar.activation(r_ex[:, :, :], r_sh[:, :, :], ACT.Exp).then_inc(r_exp, 1)

            def experts(k):
                def step(s, u):
                    j, v = s - 3, (u + 1) % 2
                    if has(j, NJ):
                        n = NJ * k + j
                        act.wait_ge(f_h_ps, n + 1)
                        wait(act, f_y_ps, NJ * k if fixed(j) and j < 2 else n - 1)
                        for c in range(FC):
                            last = nc.scalar.activation(hT[:, v, c, :], PS[:, v, c * P:(c + 1) * P], ACT.Gelu,
                                                        bias=w1b1[:, v, F + c:F + c + 1])
                        last.then_inc(f_gelu, 1)

                peeled(step, 0, 8)
                turns(act, step, 8, 22)
                peeled(step, 22, NJ + 5)

            def attn_b(s, u):
                hb, fb, v = s - 1, s - 2, (u + 1) % 2
                for h in range(H):
                    if has(hb):
                        cnt = hb * H + h
                        act.wait_ge(b_g_ps, cnt + 1)
                        wait(act, b_s_ps, cnt - 1)
                        nc.scalar.copy(gT[:, h % 2, :], PS[:, 4 + h % 2, 0:M]).then_inc(b_g, 1)
                        if h < 4:
                            act.wait_ge(b_v_ps, hb * 4 + (h + 1))
                            if h == 0:
                                wait(act, b_av, (hb - 1) * H)
                            nc.scalar.copy(vb[:, v, h % 2, (h // 2) * 512:(h // 2) * 512 + 512],
                                           PS[:, 6, :]).then_inc(b_v, 1)
                    b, hh = (hb, h - 1) if h >= 1 else (fb, H - 1)
                    if has(b):
                        cnt = b * H + hh
                        act.wait_ge(b_nb, cnt + 1)
                        wait(act, b_pT_ps, cnt - 3)
                        wait(act, b_rinv, cnt - 3)
                        r = hh % 4
                        nc.scalar.activation(pb[:, r, 0:P], PS[:, hh % 2, 0:P], ACT.Exp, bias=nbb[:, r, 0:1],
                                             scale=SCALE_B, accum_out=rsb[:, r, 0:1])
                        nc.scalar.activation(pb[:, r, P:3 * P], PS[:, hh % 2, P:3 * P], ACT.Exp, bias=nbb[:, r, 1:2],
                                             scale=SCALE_B, accum_out=rsb[:, r, 1:2]).then_inc(b_exp, 1)
                    if h == 10 and has(fb):
                        router_copies(fb + NB, TPB * fb, u, 6)
                    if h == 13 and has(s):
                        act.wait_ge(b_xT_ps, s + 1)
                        wait(act, b_s_ps, (s - 1) * H)
                        nc.scalar.copy(xnT[:, u, :], PS[:, 6, 0:M]).then_inc(b_xT, 1)

            peeled(attn_a, 0, 8)
            turns(act, attn_a, 8, 14)
            route(0)
            turns(act, attn_a, 14, 16)
            peeled(attn_a, 16, NB + 5)
            route(1)
            for q in range(4):
                act.wait_ge(b_qk_ps, q + 1)
                nc.scalar.copy(QK[:, 4 * q:4 * q + 4, :],
                               PS[:, q, :].rearrange("p (h d) -> p h d", h=4)).then_inc(b_qk, 1)
            experts(0)
            experts(1)
            peeled(attn_b, 0, 4)
            turns(act, attn_b, 4, 10)
            route(2)
            turns(act, attn_b, 10, 16)
            peeled(attn_b, 16, 18)
            route(3)
            experts(2)
            experts(3)

        @block.vector
        def _(dve):
            dve.wait_ge(s_cst, 16)
            nc.vector.tensor_copy(identb[:, :], CST[:, C_ID:C_ID + P])
            nc.vector.tensor_copy(upperb[:, :], CST[:, C_UP:C_UP + P])
            nc.vector.tensor_copy(onesb[:, :], CST[:, C_ONE:C_ONE + P])
            nc.vector.tensor_copy(maskb[:, :], CST[:, C_MASK:C_MASK + P])
            nc.vector.memset(half[:, :], -0.5).then_inc(s_castb, 1)

            def norm_stats(ln, n, tile, slot):
                dve.sem_inc(dve_waited)
                for i in range(TPB):
                    last = nc.vector.bn_stats(ln["stats"][:, slot, i, :], X[:, ds(tile + i), :])
                last.then_inc(ln["s_stats"], 1)
                dve.wait_ge(ln["s_stats"], n + 1)
                dve.sem_inc(dve_waited)
                for i in range(TPB):
                    last = nc.vector.bn_aggr(ln["mv"][:, slot, i, :], ln["stats"][:, slot, i, :])
                last.then_inc(ln["s_mv"], 1)
                dve.wait_ge(ln["s_mv"], n + 1)
                nc.vector.tensor_scalar(ln["var"][:, slot, :], ln["mv"][:, slot, :, 1], EPS, None,
                                        ALU.add).then_inc(ln["s_var"], 1)

            def norm_apply(ln, n, tile, slot):
                dve.wait_ge(ln["s_rstd"], n + 1)
                for i in range(TPB):
                    last = nc.vector.tensor_scalar(ln["out"][:, slot, i, :], X[:, ds(tile + i), :],
                                                   ln["mv"][:, slot, i, 0:1], ln["rstd"][:, slot, i:i + 1],
                                                   ALU.subtract, ALU.mult)
                last.then_inc(ln["s_out"], 1)

            def logits(n, tile, bank):
                dve.wait_ge(r_lg_ps, n + 1)
                nc.vector.tensor_tensor(LG[:, ds(tile, TPB), :],
                                        PS[:, bank, M:M + TPB * E].rearrange("p (t e) -> p t e", t=TPB),
                                        BRS[:, None, :].to_broadcast([P, TPB, E]), ALU.add).then_inc(r_lg, 1)

            def attn_a(s, u):
                v = (u + 1) % 2
                if fixed(s) and s == 0:
                    dve.wait_ge(s_x0, 16)
                if fixed(s) and s == 2:
                    dve.wait_ge(s_x1, 16)
                b = s - 4
                if has(b):
                    dve.wait_ge(a_out_ps, b + 1)
                    dve.wait_ge(a_rinv, b + 1)
                    for i in range(TPB):
                        last = nc.vector.scalar_tensor_tensor(
                            out=X[:, ds(TPB * b + i), :], in0=PS[:, 6, i * D:(i + 1) * D], scalar=ria[:, u, i:i + 1],
                            in1=X[:, ds(TPB * b + i), :], op0=ALU.mult, op1=ALU.add)
                    last.then_inc(a_x, 1)
                if has(s):
                    if not fixed(s) or s >= 2:
                        dve.wait_ge(a_xT_ps, s - 1)
                    norm_stats(LN["A"], s, TPB * s, u)
                if has(b):
                    dve.wait_ge(a_x, b + 1)
                    wait(dve, r_tok, b - 1)
                    norm_stats(LN["F"], b, TPB * b, u)
                b = s - 3
                if has(b):
                    dve.wait_ge(a_exp, b + 1)
                    nc.vector.reciprocal(ria[:, v, :], rsa[:, v, :]).then_inc(a_rinv, 1)
                b = s - 2
                if has(b):
                    dve.wait_ge(a_scores, b + 1)
                    wait(dve, a_exp, b - 1)
                    nc.vector.reduce_max(mxa[:, u, :], PS[:, 2, :].rearrange("p (t m) -> p t m", t=TPB),
                                         AX.X).then_inc(a_max, 1)
                    dve.wait_ge(a_max, b + 1)
                    nc.vector.tensor_scalar(nba[:, u, :], mxa[:, u, :], -SCALE_A, None, ALU.mult).then_inc(a_nb, 1)
                if has(s):
                    norm_apply(LN["A"], s, TPB * s, u)
                b = s - 4
                if has(b):
                    norm_apply(LN["F"], b, TPB * b, u)
                b = s - 1
                if has(b):
                    dve.wait_ge(a_qk_ps, b + 1)
                    if fixed(b) and b == 0:
                        dve.wait_ge(s_wa, 48)
                    wait(dve, a_rope, b)
                    for i in range(2):
                        last = nc.vector.tensor_tensor(rot[:, i, :], PS[:, i, :], ROPE[:, i, :], ALU.mult)
                    last.then_inc(a_rot, 1)
                    dve.wait_ge(a_rot, b + 1)
                    wait(dve, a_scores, b - 1)
                    nc.vector.tensor_tensor(qk[:, v, :, :].rearrange("p a m -> p (a m)"), rot[:, 0, :], rot[:, 1, :],
                                            ALU.add).then_inc(a_rope, 1)
                b = s - 5
                if has(b):
                    if fixed(b) and b == 0:
                        dve.wait_ge(s_wr, 32)
                    logits(b, TPB * b, 7)

            def route(k):
                g = k % GROUPS
                t0 = g * GT
                lg = LG[:, t0:t0 + GT, :]
                done = [STEPS * k]

                def then(ins):
                    done[0] += 1
                    ins.then_inc(r_step, 1)
                    dve.wait_ge(r_step, done[0])

                def over_e(ap):
                    return ap.unsqueeze(2).to_broadcast([P, GT, E])

                dve.wait_ge(r_lg, GB * (k + 1))
                then(nc.vector.reduce_max(r_mx[:, :], lg, AX.X))
                then(nc.vector.tensor_tensor(r_sh[:, :, :], lg, over_e(r_mx[:, :]), ALU.subtract))
                then(nc.vector.tensor_tensor(r_eq[:, :, :], lg, over_e(r_mx[:, :]), ALU.is_equal))
                e8 = CST[:, C_E8:C_E8 + E]
                then(nc.vector.tensor_tensor(r_eq[:, :, :], r_eq[:, :, :], e8[:, None, :].to_broadcast([P, GT, E]),
                                             ALU.mult))
                then(nc.vector.reduce_max(r_best[:, :], r_eq[:, :, :], AX.X))
                then(nc.vector.tensor_tensor(r_hot[:, :, :].rearrange("p e t -> p t e"),
                                             e8[:, None, :].to_broadcast([P, GT, E]), over_e(r_best[:, :]),
                                             ALU.is_equal))
                dve.wait_ge(r_exp, k + 1)
                then(nc.vector.reduce_sum(r_den[:, :], r_ex[:, :, :], AX.X))
                then(nc.vector.reciprocal(GATE[:, t0:t0 + GT], r_den[:, :]))
                dve.wait_ge(r_pre_ps, k + 1)
                then(nc.vector.tensor_copy(r_ps[:, :], PS[:, 7 if k < GROUPS else 6, 0:2 * E * GT]))
                assert done[0] == STEPS * k + READ_STEP
                pre = r_ps[:, 0:E * GT].rearrange("p (e t) -> p e t", e=E)
                tot = r_ps[:, E * GT:2 * E * GT]
                then(nc.vector.tensor_tensor_scan(r_inc[:, :, :].rearrange("p e t -> p (e t)"),
                                                  CST[:, C_SCAN:C_SCAN + E * GT], tot, 0.0, ALU.mult, ALU.add))
                then(nc.vector.tensor_tensor(r_exc[:, :, :].rearrange("p e t -> p (e t)"),
                                             r_inc[:, :, :].rearrange("p e t -> p (e t)"), tot, ALU.subtract))
                then(nc.vector.tensor_scalar(r_cnt[:, :], r_inc[:, :, GT - 1], float(P - 1), None, ALU.add))
                then(nc.vector.tensor_scalar(r_cnts[:, :], r_cnt[:, :], 7, None, ALU.logical_shift_right))
                then(nc.vector.tensor_copy(r_nt[:, :], r_cnts[:, :]))
                then(nc.vector.tensor_tensor_scan(r_cum[:, :], CST[:, C_ONE:C_ONE + E], r_nt[:, :], 0.0,
                                                  ALU.mult, ALU.add))
                then(nc.vector.tensor_tensor(r_base[:, :], r_cum[:, :], r_nt[:, :], ALU.subtract))
                then(nc.vector.scalar_tensor_tensor(
                    out=r_exc[:, :, :], in0=r_base[:, :].unsqueeze(2).to_broadcast([P, E, GT]), scalar=float(P),
                    in1=r_exc[:, :, :], op0=ALU.mult, op1=ALU.add))
                then(nc.vector.tensor_tensor(r_exc[:, :, :], pre, r_exc[:, :, :], ALU.add))
                then(nc.vector.tensor_tensor(r_exc[:, :, :], r_exc[:, :, :], r_hot[:, :, :], ALU.mult))
                then(nc.vector.reduce_sum(r_pos[:, :], r_exc[:, :, :].rearrange("p e t -> p t e"), AX.X))
                then(nc.vector.tensor_copy(r_posi[:, :], r_pos[:, :]))
                then(nc.vector.tensor_scalar(r_tile[:, :], r_posi[:, :], 7, None, ALU.logical_shift_right))
                then(nc.vector.tensor_copy(r_tilef[:, :], r_tile[:, :]))
                then(nc.vector.tensor_scalar(r_pos[:, :], r_pos[:, :], float(NJ), None, ALU.mult))
                then(nc.vector.scalar_tensor_tensor(out=POS[:, t0:t0 + GT], in0=r_tilef[:, :],
                                                    scalar=float(1 - NJ * P), in1=r_pos[:, :], op0=ALU.mult,
                                                    op1=ALU.add))
                then(nc.vector.tensor_tensor(
                    r_cmp[:, :, :], CST[:, C_TILE:C_TILE + NJ * E].rearrange("p (j e) -> p j e", e=E),
                    r_cum[:, None, :].to_broadcast([P, NJ, E]), ALU.is_ge))
                then(nc.vector.reduce_sum(r_te[:, :], r_cmp[:, :, :], AX.X))
                then(nc.vector.tensor_scalar(TE[:, g, :], r_te[:, :], float(E - 1), None, ALU.min))
                assert done[0] == STEPS * (k + 1), done[0]

            def experts(k):
                g = k % GROUPS

                def ring(j):
                    return NJ * k if fixed(j) and j < 2 else NJ * k + (j - 1)

                def step(s, u):
                    v = (u + 1) % 2
                    if has(s - 5, NJ):
                        e_b2 = dve.value_load(TE[0:1, g, ds(s - 5)], min_val=0, max_val=E - 1)
                    if has(s - 2, NJ):
                        e_w1 = dve.value_load(TE[0:1, g, ds(s - 2)], min_val=0, max_val=E - 1)
                    j = s - 5
                    if has(j, NJ):
                        n = NJ * k + j
                        dve.wait_ge(f_y_ps, n + 1)
                        nc.vector.tensor_tensor(XY[:, g, ds(j), :], PS[:, 4 + v, 0:D], B2S[:, ds(e_b2), :],
                                                ALU.add).then_inc(f_y, 1)
                    j = s - 2
                    if has(j, NJ):
                        n = NJ * k + j
                        dve.wait_ge(f_xT_ps, n + 1)
                        wait(dve, f_h_ps, ring(j))
                        nc.vector.tensor_copy(xsT[:, u, :], PS[:, 2 + u, 0:P]).then_inc(f_xT, 1)
                        if fixed(j) and j == 0 and k == 0:
                            dve.wait_ge(s_w1, 32)
                        wait(dve, f_gelu, ring(j))
                        nc.vector.tensor_copy(w1b1[:, u, :], W1S[:, ds(e_w1), :]).then_inc(f_w1, 1)
                    j = s
                    if has(j, NJ):
                        for c, (j0, _) in enumerate(XCHUNKS):
                            if fixed(j) and j == j0:
                                dve.wait_ge(xs_in[k][c], 16)
                        wait(dve, f_xT_ps, ring(j))
                        nc.vector.tensor_copy(xs1[:, u, :], XY[:, g, ds(j), :]).then_inc(f_in, 1)

                peeled(step, 0, 8)
                turns(dve, step, 8, 22)
                peeled(step, 22, NJ + 5)

            def combine(tile, s_inc):
                for i in range(TPB):
                    last = nc.vector.scalar_tensor_tensor(
                        out=X[:, ds(tile + i), :], in0=TOK[:, ds(tile + i), :], scalar=GATE[:, ds(tile + i)],
                        in1=X[:, ds(tile + i), :], op0=ALU.mult, op1=ALU.add)
                if s_inc is not None:
                    last.then_inc(s_inc, 1)

            def attn_b(s, u):
                hb, fb, v = s - 1, s - 2, (u + 1) % 2
                for h in range(H):
                    if h % 2 == 0:
                        b, hh = (hb, h - 5) if h >= 5 else (fb, h - 5 + H)
                        if has(b):
                            pair = hh // 2
                            dve.wait_ge(b_av, b * H + (hh + 1))
                            if pair == 0:
                                wait(dve, b_out_ps, b - 1)
                            nc.vector.tensor_copy(yT[:, v if b is hb else u, pair, :],
                                                  PS[:, 7, 0:M]).then_inc(b_y, 1)
                    b, hh = (hb, h - 2) if h >= 2 else (fb, h - 2 + H)
                    if has(b):
                        cnt = b * H + hh
                        dve.wait_ge(b_exp, cnt + 1)
                        wait(dve, b_p, cnt - 3)
                        nc.vector.reciprocal(rib[:, hh % 4, :], rsb[:, hh % 4, :]).then_inc(b_rinv, 1)
                    b, hh = (hb, h - 1) if h >= 1 else (fb, H - 1)
                    if has(b):
                        cnt = b * H + hh
                        dve.wait_ge(b_s_ps, cnt + 1)
                        nc.vector.reduce_max(mxb[:, hh % 4, 0:1], PS[:, hh % 2, 0:P], AX.X)
                        nc.vector.reduce_max(mxb[:, hh % 4, 1:2], PS[:, hh % 2, P:3 * P], AX.X).then_inc(b_max, 1)
                        dve.wait_ge(b_max, cnt + 1)
                        nc.vector.tensor_scalar(nbb[:, hh % 4, :], mxb[:, hh % 4, :], -SCALE_B, None,
                                                ALU.mult).then_inc(b_nb, 1)
                    b, hh = (hb, h - 3) if h >= 3 else (fb, h - 3 + H)
                    if has(b):
                        cnt = b * H + hh
                        dve.wait_ge(b_pT_ps, cnt + 1)
                        wait(dve, b_av, cnt - 1)
                        nc.vector.tensor_copy(pTb[:, hh % 2, :], PS[:, 2 + hh % 2, 0:3 * P]).then_inc(b_pT, 1)
                    if h == 8 and has(fb):
                        dve.wait_ge(b_out_ps, fb + 1)
                        nc.vector.tensor_tensor(X[:, ds(TPB * fb, TPB), :],
                                                PS[:, 6, 0:TPB * D].rearrange("p (t d) -> p t d", t=TPB),
                                                X[:, ds(TPB * fb, TPB), :], ALU.add).then_inc(b_x, 1)
                        dve.wait_ge(b_x, fb + 1)
                        dve.wait_ge(r_tok, fb + (NB - 1))
                        norm_stats(LN["F"], fb + NB, TPB * fb, u)
                    if h == 9 and has(fb):
                        norm_apply(LN["F"], fb + NB, TPB * fb, u)
                    if h == 10 and has(s):
                        if fixed(s) and s in (0, GB):
                            dve.wait_ge(gathered[s // GB], 16 * GT)
                        combine(TPB * s, b_comb)
                        dve.wait_ge(b_comb, s + 1)
                        wait(dve, b_xT_ps, s - 1)
                        norm_stats(LN["B"], s, TPB * s, u)
                    if h == 12 and has(s):
                        norm_apply(LN["B"], s, TPB * s, u)
                    if h == 12 and has(fb):
                        logits(fb + NB, TPB * fb, 6)

            peeled(attn_a, 0, 8)
            turns(dve, attn_a, 8, 14)
            route(0)
            turns(dve, attn_a, 14, 16)
            peeled(attn_a, 16, NB + 5)
            route(1)
            experts(0)
            experts(1)
            peeled(attn_b, 0, 4)
            turns(dve, attn_b, 4, 8)
            peeled(attn_b, 8, 10)
            route(2)
            turns(dve, attn_b, 10, 16)
            peeled(attn_b, 16, 18)
            route(3)
            experts(2)
            experts(3)
            for k in (2, 3):
                dve.wait_ge(gathered[k], 16 * GT)
                for q in range(2):
                    for b in range(4):
                        combine(GT * (k % GROUPS) + 8 * q + TPB * b, x_done if b == 3 else None)

        @block.tensor
        def _(pe):
            mm, tr = nc.tensor.matmul, nc.tensor.transpose

            def router_T(n, slot, bank):
                pe.wait_ge(LN["F"]["s_out"], n + 1)
                for i in range(TPB):
                    last = tr(PS[:, bank, i * P:(i + 1) * P], LN["F"]["out"][:, slot, i, :], ident)
                last.then_inc(r_xT_ps, 1)

            def router(n, slot, bank):
                pe.wait_ge(r_xT, n + 1)
                for i in range(TPB):
                    last = mm(PS[:, bank, M + i * E:M + (i + 1) * E], fT[:, slot, i * P:(i + 1) * P], WRS[:, :],
                              start=True, stop=True)
                last.then_inc(r_lg_ps, 1)

            def attn_a(s, u):
                v = (u + 1) % 2
                b = s - 1
                if has(b):
                    pe.wait_ge(LN["A"]["s_out"], b + 1)
                    wait(pe, a_xT, b)
                    for i in range(TPB):
                        last = tr(PS[:, 4, i * P:(i + 1) * P], LN["A"]["out"][:, v, i, :], ident)
                    last.then_inc(a_xT_ps, 1)
                b = s - 3
                if has(b):
                    pe.wait_ge(a_exp, b + 1)
                    wait(pe, a_pT, b)
                    for kc in range(TPB):
                        for i in range(TPB):
                            last = tr(PS[:, 3, kc * M + i * P:kc * M + (i + 1) * P],
                                      pa[:, v, i, kc * P:(kc + 1) * P], ident)
                    last.then_inc(a_pT_ps, 1)
                b = s - 2
                if has(b):
                    pe.wait_ge(a_rope, b + 1)
                    wait(pe, a_exp, b)
                    for i in range(TPB):
                        last = mm(PS[:, 2, i * M:(i + 1) * M], qk[:, u, 0, i * P:(i + 1) * P], qk[:, u, 1, :],
                                  start=True, stop=True)
                    last.then_inc(a_scores, 1)
                b = s - 1
                if has(b):
                    if fixed(b) and b == 0:
                        pe.wait_ge(s_wa, 48)
                    pe.wait_ge(a_xT, b + 1)
                    wait(pe, a_rot, b)
                    for i in range(2):
                        for w in range(2):
                            last = mm(PS[:, i, w * M:(w + 1) * M], WQK[:, 2 * w + i, :], xnT[:, v, :],
                                      start=True, stop=True)
                    last.then_inc(a_qk_ps, 1)
                    wait(pe, a_v, b)
                    for i in range(TPB):
                        last = mm(PS[:, 5, i * D:(i + 1) * D], xnT[:, v, i * P:(i + 1) * P], WVA[:, :],
                                  start=True, stop=True)
                    last.then_inc(a_v_ps, 1)
                b = s - 5
                if has(b):
                    if fixed(b) and b == 0:
                        pe.wait_ge(s_wr, 32)
                    wait(pe, r_lg, b)
                    router_T(b, v, 7)
                b = s - 3
                if has(b):
                    pe.wait_ge(a_pT, b + 1)
                    pe.wait_ge(a_v, b + 1)
                    wait(pe, a_x, b)
                    for i in range(TPB):
                        for kc in range(TPB):
                            last = mm(PS[:, 6, i * D:(i + 1) * D], pTa[:, v, kc, i * P:(i + 1) * P],
                                      va[:, v, kc, :], start=kc == 0, stop=kc == TPB - 1)
                    last.then_inc(a_out_ps, 1)
                b = s - 5
                if has(b):
                    router(b, v, 7)

            def route(k):
                pe.wait_ge(r_step, STEPS * k + HOT_STEP)
                bank = 7 if k < GROUPS else 6
                if k >= GROUPS:
                    pe.wait_ge(b_xT, 10 if k == 2 else NB)
                hot = r_hot[:, :, :].rearrange("p e t -> p (e t)")
                mm(PS[:, bank, 0:E * GT], upperb[:, :], hot, start=True, stop=True)
                mm(PS[:, bank, E * GT:2 * E * GT], onesb[:, :], hot, start=True, stop=True).then_inc(r_pre_ps, 1)
                pe.wait_ge(r_step, STEPS * k + READ_STEP)

            def experts(k):
                def ring(j):
                    return NJ * k if fixed(j) and j < 2 else NJ * k + (j - 1)

                def step(s, u):
                    v = (u + 1) % 2
                    if has(s - 4, NJ):
                        e = pe.value_load(TE[0:1, k % GROUPS, ds(s - 4)], min_val=0, max_val=E - 1)
                    j = s - 1
                    if has(j, NJ):
                        n = NJ * k + j
                        pe.wait_ge(f_in, n + 1)
                        wait(pe, f_xT, ring(j))
                        tr(PS[:, 2 + v, 0:P], xs1[:, v, :], ident).then_inc(f_xT_ps, 1)
                    j = s - 3
                    if has(j, NJ):
                        n = NJ * k + j
                        pe.wait_ge(f_xT, n + 1)
                        pe.wait_ge(f_w1, n + 1)
                        wait(pe, f_gelu, ring(j))
                        for c in range(FC):
                            last = mm(PS[:, v, c * P:(c + 1) * P], w1b1[:, v, c * P:(c + 1) * P], xsT[:, v, :],
                                      start=True, stop=True)
                        last.then_inc(f_h_ps, 1)
                    j = s - 4
                    if has(j, NJ):
                        n = NJ * k + j
                        pe.wait_ge(f_gelu, n + 1)
                        wait(pe, f_y, ring(j))
                        for c in range(FC):
                            last = mm(PS[:, 4 + u, 0:D], hT[:, u, c, :], W2S[:, ds(e), c, :],
                                      start=c == 0, stop=c == FC - 1)
                        last.then_inc(f_y_ps, 1)

                pe.wait_ge(r_step, STEPS * (k + 1))
                if k == 0:
                    pe.wait_ge(s_w2, 32)
                peeled(step, 0, 8)
                turns(pe, step, 8, 22)
                peeled(step, 22, NJ + 5)

            def attn_b(s, u):
                hb, fb, v = s - 1, s - 2, (u + 1) % 2

                def scores(b, hh, slot):
                    cnt = b * H + hh
                    pe.wait_ge(b_g, cnt + 1)
                    wait(pe, b_exp, cnt - 1)
                    ps = PS[:, hh % 2, :]
                    mm(ps[:, 0:P], gT[:, hh % 2, 0:P], xnT[:, slot, 0:P], start=True, stop=False)
                    mm(ps[:, 0:P], identb[:, :], maskb[:, :], start=False, stop=True)
                    mm(ps[:, P:3 * P], gT[:, hh % 2, P:M], xnT[:, slot, :], start=True, stop=True)
                    mm(ps[:, 2 * P:3 * P], identb[:, :], maskb[:, :], start=False, stop=True,
                       skip_group_check=True).then_inc(b_s_ps, 1)

                def transposes(b, hh):
                    cnt = b * H + hh
                    pe.wait_ge(b_p, cnt + 1)
                    wait(pe, b_pT, cnt - 1)
                    for c in range(3):
                        last = tr(PS[:, 2 + hh % 2, c * P:(c + 1) * P], pb[:, hh % 4, c * P:(c + 1) * P], ident)
                    last.then_inc(b_pT_ps, 1)

                def product(b, hh, slot):
                    cnt = b * H + hh
                    pe.wait_ge(b_pT, cnt + 1)
                    if hh == 0:
                        pe.wait_ge(b_v, b * 4 + 4)
                    if hh % 2 == 0:
                        wait(pe, b_y, b * NPAIR + hh // 2)
                    q = DK * (hh % 2)
                    mm(PS[q:q + DK, 7, 0:M], vb[:, slot, 0, hh * DK:(hh + 1) * DK], pTb[:, hh % 2, 0:M],
                       start=True, stop=True)
                    last = mm(PS[q:q + DK, 7, P:M], vb[:, slot, 1, hh * DK:(hh + 1) * DK], pTb[:, hh % 2, M:3 * P],
                              start=False, stop=True, skip_group_check=True)
                    last.then_inc(b_av, 1)

                for h in range(H):
                    if has(hb):
                        cnt = hb * H + h
                        if h == 0:
                            pe.wait_ge(b_xT, hb + 1)
                        wait(pe, b_g, cnt - 1)
                        mm(PS[:, 4 + h % 2, 0:M], QK[:, h, :], xnT[:, v, :], start=True, stop=True).then_inc(b_g_ps, 1)
                        if h < 4:
                            if h > 0:
                                pe.wait_ge(b_v, hb * 4 + h)
                            i, c = h % 2, h // 2
                            mm(PS[:, 6, :], xnT[:, v, i * P:(i + 1) * P], WVB[:, c * 512:(c + 1) * 512],
                               start=True, stop=True).then_inc(b_v_ps, 1)
                    if h >= 1 and has(hb):
                        scores(hb, h - 1, v)
                    if h == 0 and has(fb):
                        scores(fb, H - 1, u)
                    if h >= 3 and has(hb):
                        transposes(hb, h - 3)
                    if h < 3 and has(fb):
                        transposes(fb, h - 3 + H)
                    if h >= 4 and has(hb):
                        product(hb, h - 4, v)
                    if h < 4 and has(fb):
                        product(fb, h - 4 + H, u)
                    if h in (6, 7) and has(fb):
                        i = h - 6
                        if i == 0:
                            pe.wait_ge(b_y, fb * NPAIR + NPAIR)
                            if has(hb):
                                pe.wait_ge(b_v, hb * 4 + 4)
                        for pair in range(NPAIR):
                            last = mm(PS[:, 6, i * D:(i + 1) * D], yT[:, u, pair, i * P:(i + 1) * P], WO[:, pair, :],
                                      start=pair == 0, stop=pair == NPAIR - 1)
                        if i == 1:
                            last.then_inc(b_out_ps, 1)
                    if h == 10 and has(fb):
                        router_T(fb + NB, u, 6)
                    if h == 11 and has(fb):
                        router(fb + NB, u, 6)
                    if h == 13 and has(s):
                        pe.wait_ge(LN["B"]["s_out"], s + 1)
                        if has(fb):
                            pe.wait_ge(r_lg, fb + (NB + 1))
                        elif has(hb):
                            pe.wait_ge(b_v, hb * 4 + 4)
                        for i in range(TPB):
                            last = tr(PS[:, 6, i * P:(i + 1) * P], LN["B"]["out"][:, u, i, :], ident)
                        last.then_inc(b_xT_ps, 1)

            pe.wait_ge(s_cst, 16)
            pe.wait_ge(s_castb, 1)
            peeled(attn_a, 0, 8)
            turns(pe, attn_a, 8, 14)
            route(0)
            turns(pe, attn_a, 14, 16)
            peeled(attn_a, 16, NB + 5)
            route(1)
            pe.wait_ge(s_wb, 64)
            for h in range(H):
                last = mm(PS[:, h // 4, (h % 4) * P:(h % 4 + 1) * P], WQB[:, h, :], WKB[:, h, :],
                          start=True, stop=True)
                if h % 4 == 3:
                    last.then_inc(b_qk_ps, 1)
            pe.wait_ge(b_qk, 4)
            experts(0)
            experts(1)
            pe.wait_ge(f_y, 2 * NJ)
            peeled(attn_b, 0, 4)
            turns(pe, attn_b, 4, 10)
            route(2)
            turns(pe, attn_b, 10, 16)
            peeled(attn_b, 16, 18)
            route(3)
            experts(2)
            experts(3)


STEPS, SHIFT_STEP, HOT_STEP, READ_STEP = 28, 2, 6, 9

_OUT = (NB, M, D)


def tables():
    i = np.arange(D // 2, dtype=np.float32)
    theta = np.power(np.float32(10000.0), (np.float32(-2.0) * (i - np.float32(1.0)) / np.float32(D)).astype(np.float32))
    ang = (np.arange(M, dtype=np.float32)[:, None] * theta[None, :].astype(np.float32)).astype(np.float32)
    cos, sin = np.cos(ang).T, np.sin(ang).T
    rope = np.zeros((P, 2, 2, M), np.float32)
    rope[0::2, 0], rope[1::2, 0] = cos[:, None, :], cos[:, None, :]
    rope[0::2, 1], rope[1::2, 1] = sin[:, None, :], -sin[:, None, :]
    cst = np.zeros((P, C_W), np.float32)
    r = np.arange(P)
    cst[:, C_ID:C_ID + P] = np.eye(P)
    cst[:, C_UP:C_UP + P] = r[:, None] < r[None, :]
    cst[:, C_ONE:C_ONE + P] = 1.0
    cst[:, C_MASK:C_MASK + P] = np.where(r[:, None] < r[None, :], MASKED, 0.0)
    cst[:, C_E8:C_E8 + E] = E - np.arange(E)
    cst[:, C_SCAN:C_SCAN + E * GT] = (np.arange(E * GT) % GT != 0)
    cst[:, C_TILE:C_TILE + NJ * E] = np.arange(NJ * E) // E
    return rope.reshape(P, 2, 2 * M), cst


def kernel(**inputs):
    import concourse.bacc as _bacc
    from concourse.bass_utils import run_bass_kernel_spmd as _run

    a = {n.replace("L0_", ""): np.asarray(v) for n, v in inputs.items()}
    swap = np.arange(D) ^ 1
    wq, wk = a["attn_a_wq"].T, a["attn_a_wk"].T
    rope, cst = tables()
    arrays = {
        "x": a["attn_a_x"],
        "wqk_a": np.stack([wq, wq[:, swap], wk, wk[:, swap]], axis=1),
        "wv_a": a["attn_a_wv"].T,
        "rope": rope,
        "w_q": a["attn_b_w_q"],
        "w_k": a["attn_b_w_k"],
        "wv_b": a["attn_b_w_v"].reshape(H * DK, D).T,
        "w_o": a["attn_b_w_o"],
        "W1": a["ffn_W1"],
        "b1t": a["ffn_b1"].reshape(E, FC, P).transpose(2, 0, 1),
        "W2": a["ffn_W2"],
        "b2": a["ffn_b2"],
        "Wr": a["ffn_Wr"],
        "br": a["ffn_br"],
        "cst": cst,
    }
    arrays = {f"in_{n}": np.ascontiguousarray(v) for n, v in arrays.items()}
    nc = _bacc.Bacc("TRN2", target_bir_lowering=False, num_devices=1)
    args = [nc.dram_tensor(n, v.shape, mybir.dt.from_np(v.dtype), kind="ExternalInput").ap()
            for n, v in arrays.items()]
    out = nc.dram_tensor("out_dram", _OUT, F32, kind="ExternalOutput").ap()
    build(nc, *args, out)
    r = _run(nc, [arrays], core_ids=[0])
    return r.results[0]["out_dram"]
```

```python
from contextlib import ExitStack

import numpy as np
import concourse.bass as bass
from concourse import mybir

F32 = mybir.dt.float32
F32R = mybir.dt.float32r
BF16 = mybir.dt.bfloat16
I32 = mybir.dt.int32
ALU = mybir.AluOpType
ACT = mybir.ActivationFunctionType
AX = mybir.AxisListType

P = 128
NB, M, D = 16, 256, 128
TPB = M // P
NT = NB * TPB
H, DK = 16, 64
NPAIR = H // 2
E, F = 8, 512
FC = F // P
GROUPS = 2
GB = NB // GROUPS
GT = GB * TPB
NJ = GT + E - 1
NL = GROUPS * NJ
W1W = F + FC
W2W = FC * D + D
RING = 4
EPS = 1e-5
SCALE_A = float(1.0 / np.sqrt(np.float32(D)))
SCALE_B = float(1.0 / np.sqrt(np.float32(DK)))
MASKED, LOWEST = -3.0e38, -3.4e38
YCHUNKS = ((0, 6), (6, 12), (12, 18), (18, NJ))
XCHUNKS = ((0, 4), (4, NJ))

C_ID, C_UP, C_ONE = 0, P, 2 * P
C_ZERO, C_MASK = 3 * P, 4 * P
C_E8 = 5 * P
C_SCAN = C_E8 + E
C_TILE = C_SCAN + E * GT
C_W = C_TILE + NJ * E


def one_pass(ap):
    return ap.bitcast(F32R)


def ds(i, n=1):
    return bass.ds(i, n)


def fixed(v):
    return isinstance(v, int)


def wait(eng, sem, value):
    if not fixed(value) or value > 0:
        eng.wait_ge(sem, value)


def turns(eng, body, first, last, n=2):
    assert first % n == 0 and last % n == 0
    with eng.Fori(first // n, last // n) as turn:
        for u in range(n):
            body(turn * n + u, u)


def peeled(body, first, last, n=2):
    for s in range(first, last):
        body(s, s % n)


def expert_steps(eng, step):
    second = NJ // RING * RING
    peeled(step, 0, 2 * RING, RING)
    turns(eng, step, 2 * RING, second, RING)
    peeled(step, second, second + RING, RING)
    turns(eng, step, second + RING, NL // RING * RING, RING)
    peeled(step, NL // RING * RING, NL + 5, RING)


def has(b, n=NB):
    return not fixed(b) or 0 <= b < n


def build(nc, x, wqk_a, wv_a, rope, w_q, w_k, wv_b, w_o, W1, b1t, W2, b2, Wr, br, cst, out):
    ctx = ExitStack()
    with ctx:
        def sb(name, shape, dt=F32):
            return ctx.enter_context(nc.sbuf_tensor(name, shape, dt))

        def sem(name):
            return ctx.enter_context(nc.semaphore(name))

        xs_dram = [nc.dram_tensor(f"xs_dram{g}", [P * NJ, D], F32, kind="Internal").ap() for g in range(GROUPS)]
        ys_dram = [nc.dram_tensor(f"ys_dram{g}", [P * NJ, D], F32, kind="Internal").ap() for g in range(GROUPS)]

        X = sb("X", [P, NT, D])
        CST = sb("CST", [P, C_W])
        ident = CST[:, C_ID:C_ID + P]
        upperb = sb("upperb", [P, P], BF16)
        onesb = sb("onesb", [P, P], BF16)
        half = sb("half", [P, TPB])
        WQK = sb("WQK", [P, 4, D])
        WVA = sb("WVA", [P, D])
        ROPE = sb("ROPE", [P, 2, 2 * M])
        QKh, QKl = (sb(n, [P, H, D]) for n in ("QKh", "QKl"))
        WVBh, WVBl = (sb(n, [P, H * DK]) for n in ("WVBh", "WVBl"))
        WO = sb("WO", [P, NPAIR, D])
        W1S = sb("W1S", [P, E, W1W])
        W2S = sb("W2S", [P, E, W2W])
        WRS = sb("WRS", [P, E])
        BRS = sb("BRS", [P, E])
        LN = {}
        for n in "AFB":
            LN[n] = {
                "stats": sb(f"stats{n}", [P, 2, TPB, 6]), "mv": sb(f"mv{n}", [P, 2, TPB, 2]),
                "var": sb(f"var{n}", [P, 2, TPB]), "rstd": sb(f"rstd{n}", [P, 2, TPB]),
                "out": sb(f"ln{n}", [P, 2, TPB, D]),
                "s_stats": sem(f"ln{n}_stats"), "s_mv": sem(f"ln{n}_mv"), "s_var": sem(f"ln{n}_var"),
                "s_rstd": sem(f"ln{n}_rstd"), "s_out": sem(f"ln{n}_out"),
            }
        xnT = sb("xnT", [P, 2, M])
        qks = sb("qks", [P, 2 * M])
        va = sb("va", [P, 2, TPB, D])
        mxa, nba, rsa, ria = (sb(n, [P, 2, TPB]) for n in ("mxa", "nba", "rsa", "ria"))
        xh, xl = (sb(n, [P, 2, M]) for n in ("xh", "xl"))
        gT = sb("gT", [P, 2, M])
        mxb, nbb, rsb, rib = (sb(n, [P, 4, TPB]) for n in ("mxb", "nbb", "rsb", "rib"))
        pb = sb("pb", [P, 4, 3 * P])
        pTb = sb("pTb", [P, 2, 3 * P])
        vb = sb("vb", [P, 2, TPB, H * DK])
        rot = vb[:, 0, 0, :].rearrange("p (a m) -> p a m", a=2)
        qk = vb[:, 0, 1, :].rearrange("p (a b m) -> p a b m", a=2, b=2)
        pa = vb[:, 1, 0, :].rearrange("p (a b m) -> p a b m", a=2, b=TPB)
        pTa = vb[:, 1, 1, :].rearrange("p (a b m) -> p a b m", a=2, b=TPB)
        yT = sb("yT", [P, 2, NPAIR, M])
        WQB = yT[0:DK, 0, :, :].rearrange("p a (c d) -> p (a c) d", c=2)
        WKB = yT[0:DK, 1, :, :].rearrange("p a (c d) -> p (a c) d", c=2)
        WVB = pb.rearrange("p a b -> p (a b)")[:, 0:H * DK]
        yflat = yT.rearrange("p a b m -> p (a b m)")
        w2b2 = yflat[:, 0:RING * W2W].rearrange("p (r w) -> p r w", r=RING)
        hT = yflat[:, RING * W2W:RING * W2W + 2 * F].rearrange("p (a c t) -> p a c t", a=2, c=FC)
        TOK = sb("TOK", [P, NT, D])
        fT = sb("fT", [P, 2, M])
        LG = sb("LG", [P, NT, E])
        GATE = sb("GATE", [P, NT])
        POS = sb("POS", [P, NT], I32)
        TE = sb("TE", [P, NL], I32)
        r_mx = sb("r_mx", [P, GT])
        r_sh = sb("r_sh", [P, GT, E])
        r_ex = sb("r_ex", [P, GT, E])
        r_den = sb("r_den", [P, GT])
        r_eq = sb("r_eq", [P, GT, E])
        r_best = sb("r_best", [P, GT])
        r_ps = sb("r_ps", [P, 2 * E * GT])
        r_hot = sb("r_hot", [P, E, GT], BF16)
        r_inc = sb("r_inc", [P, E, GT])
        r_exc = sb("r_exc", [P, E, GT])
        r_cnt = sb("r_cnt", [P, E], I32)
        r_cnts = sb("r_cnts", [P, E], I32)
        r_nt = sb("r_nt", [P, E])
        r_cum = sb("r_cum", [P, E])
        r_base = sb("r_base", [P, E])
        r_pos = sb("r_pos", [P, GT])
        r_posi = sb("r_posi", [P, GT], I32)
        r_tile = sb("r_tile", [P, GT], I32)
        r_tilef = sb("r_tilef", [P, GT])
        r_cmp = sb("r_cmp", [P, NJ, E])
        r_te = sb("r_te", [P, NJ])
        XY = sb("XY", [P, NL, D])
        xs1 = sb("xs1", [P, 2, D])
        w1b1 = sb("w1b1", [P, 2, W1W])
        xsT = sb("xsT", [P, 2, P])
        PS = ctx.enter_context(nc.psum_tensor("PS", [P, 8, 512], F32))

        s_cst, s_x0, s_x1, s_wa, s_wb, s_wr, s_w1, s_w2, s_xs0 = (
            sem(n) for n in ("cst_in", "x_first_in", "x_rest_in", "w_attn_a_in", "w_attn_b_in", "w_router_in",
                             "w1_in", "w2_in", "xs_zeroed"))
        s_castb, s_zero = sem("consts_cast"), sem("zeros_set")
        (a_xT_ps, a_xT, a_qk_ps, a_qks, a_sin, a_rot, a_rope, a_v_ps, a_v, a_scores, a_max, a_nb, a_exp, a_rinv, a_pT_ps, a_pT,
         a_out_ps, a_x) = (sem("a_" + n) for n in (
             "xT_ps", "xT", "qk_ps", "qks", "sin", "rot", "rope", "v_ps", "v", "scores", "max", "nb", "exp", "rinv", "pT_ps", "pT",
             "out_ps", "x"))
        r_xT_ps, r_xT, r_tok, r_lg_ps, r_lg = (sem("r_" + n) for n in ("xT_ps", "xT", "tok", "lg_ps", "lg"))
        r_step, r_exp, r_pre_ps = (sem("r_" + n) for n in ("step", "exp", "pre_ps"))
        scattered = [sem(f"scattered{k}") for k in range(4)]
        gathered = [sem(f"gathered{k}") for k in range(4)]
        last_gathered = [sem(f"last_gathered{q}") for q in range(4)]
        xs_in = [[sem(f"xs_in{k}_{c}") for c in range(len(XCHUNKS))] for k in range(4)]
        ys_out = [sem(f"ys_out{k}") for k in range(4)]
        f_in, f_xT_ps, f_xT, f_w, f_h_ps, f_gelu, f_y_ps, f_y = (
            sem("f_" + n) for n in ("in", "xT_ps", "xT", "w", "h_ps", "gelu", "y_ps", "y"))
        b_qk_ps, b_qk, b_qkl, b_wv = (sem(n) for n in ("b_qk_ps", "b_qk", "b_qkl", "b_wv"))
        b_comb, b_xT_ps, b_xT, b_xl, b_v_ps, b_v, b_out_ps, b_x = (
            sem("b_" + n) for n in ("comb", "xT_ps", "xT", "xl", "v_ps", "v", "out_ps", "x"))
        b_g_ps, b_g, b_s_ps, b_max, b_nb, b_exp, b_rinv, b_p, b_pT_ps, b_pT, b_av, b_y = (
            sem("b_h" + n) for n in ("g_ps", "g", "s_ps", "max", "nb", "exp", "rinv", "p", "pT_ps", "pT", "av", "y"))
        dve_waited, pool_waited = sem("dve_waited"), sem("pool_waited")
        x_done, s_out = sem("x_done"), sem("out_stored")

        block = ctx.enter_context(nc.Block())

        @block.sync
        def _(sp):
            xv = x.rearrange("b (t p) d -> p (b t) d", p=P)
            sp.dma_start(CST[:, :], cst).then_inc(s_cst, 16)
            sp.dma_start(X[:, 0:4, :], xv[:, 0:4, :]).then_inc(s_x0, 16)
            sp.dma_start(WQK[:, :, :], wqk_a).then_inc(s_wa, 16)
            sp.dma_start(ROPE[:, :, :], rope).then_inc(s_wa, 16)
            sp.dma_start(WVA[:, :], wv_a).then_inc(s_wa, 16)
            sp.dma_start(WRS[:, :], Wr).then_inc(s_wr, 16)
            sp.dma_start(BRS[:, :], br.rearrange("(a e) -> a e", a=1).to_broadcast([P, E])).then_inc(s_wr, 16)
            sp.dma_start(X[:, 4:NT, :], xv[:, 4:NT, :]).then_inc(s_x1, 16)
            sp.wait_ge(s_zero, 1)
            for g in range(GROUPS):
                sp.dma_start(xs_dram[g].rearrange("(p j) d -> p j d", p=P), XY[:, g * NJ:(g + 1) * NJ, :]).then_inc(s_xs0, 16)
            sp.dma_start(W1S[:, :, 0:F], W1.rearrange("e d f -> d e f")).then_inc(s_w1, 16)
            sp.dma_start(W1S[:, :, F:W1W], b1t).then_inc(s_w1, 16)
            for c in range(FC):
                sp.dma_start(W2S[:, :, c * D:(c + 1) * D],
                             W2[:, c * P:(c + 1) * P, :].rearrange("e p d -> p e d")).then_inc(s_w2, 16)
            sp.dma_start(W2S[:, :, FC * D:W2W], b2.rearrange("(a e) d -> a e d", a=1).to_broadcast([P, E, D])
                         ).then_inc(s_w2, 16)
            sp.dma_start(WQB, w_q.rearrange("h k c -> k h c")).then_inc(s_wb, 16)
            sp.dma_start(WKB, w_k.rearrange("h k c -> k h c")).then_inc(s_wb, 16)
            sp.dma_start(WVB, wv_b).then_inc(s_wb, 16)
            sp.dma_start(WO[:, :, :], w_o.rearrange("(a p) d -> p a d", p=P)).then_inc(s_wb, 16)
            for k in range(4):
                g = k % GROUPS
                xsv = xs_dram[g].rearrange("(p j) d -> p j d", p=P)
                ysv = ys_dram[g].rearrange("(p j) d -> p j d", p=P)
                sp.wait_ge(scattered[k], 16 * GT)
                if k >= GROUPS:
                    sp.wait_ge(gathered[k - GROUPS], 16 * GT)
                for c, (j0, j1) in enumerate(XCHUNKS):
                    sp.dma_start(XY[:, g * NJ + j0:g * NJ + j1, :], xsv[:, j0:j1, :]).then_inc(xs_in[k][c], 16)
                if k % 2 == 1:
                    for kk in (k - 1, k):
                        gg = kk % GROUPS
                        yv = ys_dram[gg].rearrange("(p j) d -> p j d", p=P)
                        for j0, j1 in YCHUNKS:
                            sp.wait_ge(f_y, NJ * kk + j1)
                            sp.dma_start(yv[:, j0:j1, :], XY[:, gg * NJ + j0:gg * NJ + j1, :]).then_inc(ys_out[kk], 16)
            ov = out.rearrange("b (t p) d -> p (b t) d", p=P)
            for q in range(8):
                sp.wait_ge(x_done, q + 1)
                sp.dma_start(ov[:, 4 * q:4 * q + 4, :], X[:, 4 * q:4 * q + 4, :]).then_inc(s_out, 16)
            sp.wait_ge(s_out, 8 * 16)

        @block.gpsimd
        def _(pool):
            nc.gpsimd.memset(XY[:, :, :], 0.0).then_inc(s_zero, 1)
            pool.wait_ge(s_castb, 1)

            def rstd(ln, n, slot):
                pool.wait_ge(ln["s_var"], n + 1)
                nc.gpsimd.tensor_tensor(ln["rstd"][:, slot, :], ln["var"][:, slot, :], half[:, :],
                                        ALU.pow).then_inc(ln["s_rstd"], 1)

            def scatter(k, t):
                tile = GT * (k % GROUPS) + t
                nc.gpsimd.indirect_dma_start(
                    out=xs_dram[k % GROUPS], out_offset=bass.IndirectOffsetOnAxis(ap=POS[:, tile:tile + 1], axis=0),
                    in_=TOK[:, tile, :], in_offset=None).then_inc(scattered[k], 16)

            def before_scatters(k):
                pool.wait_ge(r_step, STEPS * (k + 1))
                pool.wait_ge(r_tok, GB * (k + 1))
                if k < GROUPS:
                    pool.wait_ge(s_xs0, 32)
                else:
                    for c in range(len(XCHUNKS)):
                        pool.wait_ge(xs_in[k - GROUPS][c], 16)

            def gather(k, t):
                tile = GT * (k % GROUPS) + t
                nc.gpsimd.indirect_dma_start(
                    out=TOK[:, tile, :], out_offset=None, in_=ys_dram[k % GROUPS],
                    in_offset=bass.IndirectOffsetOnAxis(ap=POS[:, tile:tile + 1], axis=0)
                ).then_inc(gathered[k] if k < 3 else last_gathered[t // 4], 16)

            def attn_a(s, u):
                if has(s):
                    rstd(LN["A"], s, u)
                if has(s - 4):
                    rstd(LN["F"], s - 4, u)
                b = s - 1
                if has(b):
                    pool.wait_ge(a_qks, b + 1)
                    wait(pool, a_rope, b)
                    if fixed(b) and b == 0:
                        pool.wait_ge(s_wa, 48)
                    nc.gpsimd.tensor_tensor(rot[:, 1, :], qks[:, :], ROPE[:, 1, :], ALU.mult).then_inc(a_sin, 1)

            peeled(attn_a, 0, 8)
            turns(pool, attn_a, 8, 14)
            for s in range(14, NB + 5):
                attn_a(s, s % 2)
                if s == 14:
                    before_scatters(0)
                for t in range(3 * (s - 14), min(3 * (s - 13), GT)):
                    scatter(0, t)
            before_scatters(1)
            for t in range(GT):
                scatter(1, t)
            pool.wait_ge(ys_out[0], 16 * len(YCHUNKS))
            for t in range(GT):
                gather(0, t)

            def attn_b(s, u, more=None):
                hb, fb = s - 1, s - 2
                for h in range(H):
                    b, hh = (hb, h - 2) if h >= 2 else (fb, h - 2 + H)
                    if has(b):
                        pool.wait_ge(b_rinv, b * H + (hh + 1))
                        pool.sem_inc(pool_waited)
                        nc.gpsimd.tensor_scalar(pb[:, hh % 4, 0:P], pb[:, hh % 4, 0:P], rib[:, hh % 4, 0:1], 1.0,
                                                ALU.mult, ALU.mult)
                        nc.gpsimd.tensor_scalar(pb[:, hh % 4, P:3 * P], pb[:, hh % 4, P:3 * P], rib[:, hh % 4, 1:2],
                                                1.0, ALU.mult, ALU.mult).then_inc(b_p, 1)
                    if h == 8 and has(fb):
                        rstd(LN["F"], fb + NB, u)
                    if h == 10 and has(s):
                        rstd(LN["B"], s, u)
                    if more is not None:
                        more(h)

            def gather1(h):
                if h == 0:
                    pool.wait_ge(ys_out[1], 16 * len(YCHUNKS))
                gather(1, h)

            def scatter2(h):
                if h == 0:
                    before_scatters(2)
                scatter(2, h)

            attn_b(0, 0)
            attn_b(1, 1, gather1)
            peeled(attn_b, 2, 4)
            turns(pool, attn_b, 4, 10)
            attn_b(10, 0)
            attn_b(11, 1, scatter2)
            turns(pool, attn_b, 12, 16)
            peeled(attn_b, 16, 18)
            before_scatters(3)
            for t in range(GT):
                scatter(3, t)
            for k in (2, 3):
                pool.wait_ge(ys_out[k], 16 * len(YCHUNKS))
                for t in range(GT):
                    gather(k, t)

        @block.scalar
        def _(act):
            def router_copies(n, tile, slot, bank):
                act.wait_ge(LN["F"]["s_out"], n + 1)
                nc.scalar.copy(TOK[:, ds(tile, TPB), :], LN["F"]["out"][:, slot, :, :]).then_inc(r_tok, 1)
                act.wait_ge(r_xT_ps, n + 1)
                wait(act, r_lg_ps, n - 1)
                nc.scalar.copy(fT[:, slot, :], PS[:, bank, 0:M]).then_inc(r_xT, 1)

            def attn_a(s, u):
                v = (u + 1) % 2
                b = s - 1
                if has(b):
                    act.wait_ge(a_xT_ps, b + 1)
                    wait(act, a_v_ps, b - 1)
                    nc.scalar.copy(xnT[:, v, :], PS[:, 4, 0:M]).then_inc(a_xT, 1)
                b = s - 5
                if has(b):
                    router_copies(b, TPB * b, v, 7)
                b = s - 3
                if has(b):
                    act.wait_ge(a_pT_ps, b + 1)
                    wait(act, a_out_ps, b - 1)
                    nc.scalar.copy(pTa[:, v, :, :], PS[:, 3, :].rearrange("p (t m) -> p t m", t=TPB)).then_inc(a_pT, 1)
                b = s - 1
                if has(b):
                    act.wait_ge(a_qk_ps, b + 1)
                    wait(act, a_sin, b)
                    nc.scalar.copy(qks[:, :], PS[:, 1, :]).then_inc(a_qks, 1)
                b = s - 2
                if has(b):
                    act.wait_ge(a_nb, b + 1)
                    wait(act, a_pT_ps, b - 1)
                    wait(act, a_rinv, b - 1)
                    for i in range(TPB):
                        last = nc.scalar.activation(pa[:, u, i, :], PS[:, 2, i * M:(i + 1) * M], ACT.Exp,
                                                    bias=nba[:, u, i:i + 1], scale=SCALE_A,
                                                    accum_out=rsa[:, u, i:i + 1])
                    last.then_inc(a_exp, 1)
                b = s - 1
                if has(b):
                    act.wait_ge(a_v_ps, b + 1)
                    wait(act, a_out_ps, b - 1)
                    nc.scalar.copy(va[:, v, :, :], PS[:, 5, 0:TPB * D].rearrange("p (t d) -> p t d", t=TPB)).then_inc(a_v, 1)

            def route(k):
                act.wait_ge(r_step, STEPS * k + SHIFT_STEP)
                nc.scalar.activation(r_ex[:, :, :], r_sh[:, :, :], ACT.Exp).then_inc(r_exp, 1)

            def experts(layer):
                n0 = NL * layer

                def ring(j):
                    return n0 if fixed(j) and j < 2 else n0 + (j - 1)

                def step(s, u):
                    w, v = u % 2, (u + 1) % 2
                    j = s - 2
                    if has(j, NL):
                        act.wait_ge(f_xT_ps, n0 + (j + 1))
                        wait(act, f_h_ps, ring(j))
                        nc.scalar.copy(xsT[:, w, :], PS[:, 2 + w, 0:P]).then_inc(f_xT, 1)
                    j = s - 3
                    if has(j, NL):
                        act.wait_ge(f_h_ps, n0 + (j + 1))
                        wait(act, f_y_ps, ring(j))
                        for c in range(FC):
                            last = nc.scalar.activation(hT[:, v, c, :], PS[:, v, c * P:(c + 1) * P], ACT.Gelu,
                                                        bias=w1b1[:, v, F + c:F + c + 1])
                        last.then_inc(f_gelu, 1)

                expert_steps(act, step)

            def attn_b(s, u):
                hb, fb, v = s - 1, s - 2, (u + 1) % 2
                for h in range(H):
                    if has(hb):
                        cnt = hb * H + h
                        act.wait_ge(b_g_ps, cnt + 1)
                        wait(act, b_s_ps, cnt - 1)
                        nc.scalar.copy(gT[:, h % 2, :], PS[:, 4 + h % 2, 0:M]).then_inc(b_g, 1)
                        if h < 4:
                            act.wait_ge(b_v_ps, hb * 4 + (h + 1))
                            if h == 0:
                                wait(act, b_av, (hb - 1) * H)
                            nc.scalar.copy(vb[:, v, h % 2, (h // 2) * 512:(h // 2) * 512 + 512],
                                           PS[:, 6, :]).then_inc(b_v, 1)
                    b, hh = (hb, h - 1) if h >= 1 else (fb, H - 1)
                    if has(b):
                        cnt = b * H + hh
                        act.wait_ge(b_nb, cnt + 1)
                        wait(act, b_pT_ps, cnt - 3)
                        wait(act, b_rinv, cnt - 3)
                        r = hh % 4
                        nc.scalar.activation(pb[:, r, 0:P], PS[:, hh % 2, 0:P], ACT.Exp, bias=nbb[:, r, 0:1],
                                             scale=SCALE_B, accum_out=rsb[:, r, 0:1])
                        nc.scalar.activation(pb[:, r, P:3 * P], PS[:, hh % 2, P:3 * P], ACT.Exp, bias=nbb[:, r, 1:2],
                                             scale=SCALE_B, accum_out=rsb[:, r, 1:2]).then_inc(b_exp, 1)
                    if h == 10 and has(fb):
                        router_copies(fb + NB, TPB * fb, u, 6)
                    if h == 13 and has(s):
                        act.wait_ge(b_xT_ps, s + 1)
                        wait(act, b_s_ps, (s - 1) * H)
                        nc.scalar.copy(one_pass(xh[:, u, :]), PS[:, 6, 0:M])
                        nc.scalar.copy(xnT[:, u, :], PS[:, 6, 0:M]).then_inc(b_xT, 1)

            peeled(attn_a, 0, 8)
            turns(act, attn_a, 8, 14)
            route(0)
            turns(act, attn_a, 14, 16)
            peeled(attn_a, 16, NB + 5)
            route(1)
            for q in range(4):
                act.wait_ge(b_qk_ps, q + 1)
                nc.scalar.copy(one_pass(QKh[:, 4 * q:4 * q + 4, :]),
                               PS[:, q, :].rearrange("p (h d) -> p h d", h=4)).then_inc(b_qk, 1)
            act.wait_ge(s_wb, 64)
            nc.scalar.copy(one_pass(WVBh[:, :]), WVB).then_inc(b_wv, 1)
            experts(0)
            peeled(attn_b, 0, 4)
            turns(act, attn_b, 4, 10)
            route(2)
            turns(act, attn_b, 10, 16)
            peeled(attn_b, 16, 18)
            route(3)
            experts(1)

        @block.vector
        def _(dve):
            dve.wait_ge(s_cst, 16)
            nc.vector.tensor_copy(upperb[:, :], CST[:, C_UP:C_UP + P])
            nc.vector.tensor_copy(onesb[:, :], CST[:, C_ONE:C_ONE + P])
            nc.vector.memset(half[:, :], -0.5).then_inc(s_castb, 1)

            def norm_stats(ln, n, tile, slot):
                dve.sem_inc(dve_waited)
                for i in range(TPB):
                    last = nc.vector.bn_stats(ln["stats"][:, slot, i, :], X[:, ds(tile + i), :])
                last.then_inc(ln["s_stats"], 1)
                dve.wait_ge(ln["s_stats"], n + 1)
                dve.sem_inc(dve_waited)
                for i in range(TPB):
                    last = nc.vector.bn_aggr(ln["mv"][:, slot, i, :], ln["stats"][:, slot, i, :])
                last.then_inc(ln["s_mv"], 1)
                dve.wait_ge(ln["s_mv"], n + 1)
                nc.vector.tensor_scalar(ln["var"][:, slot, :], ln["mv"][:, slot, :, 1], EPS, None,
                                        ALU.add).then_inc(ln["s_var"], 1)

            def norm_apply(ln, n, tile, slot):
                dve.wait_ge(ln["s_rstd"], n + 1)
                for i in range(TPB):
                    last = nc.vector.tensor_scalar(ln["out"][:, slot, i, :], X[:, ds(tile + i), :],
                                                   ln["mv"][:, slot, i, 0:1], ln["rstd"][:, slot, i:i + 1],
                                                   ALU.subtract, ALU.mult)
                last.then_inc(ln["s_out"], 1)

            def logits(n, tile, bank):
                dve.wait_ge(r_lg_ps, n + 1)
                nc.vector.tensor_tensor(LG[:, ds(tile, TPB), :],
                                        PS[:, bank, M:M + TPB * E].rearrange("p (t e) -> p t e", t=TPB),
                                        BRS[:, None, :].to_broadcast([P, TPB, E]), ALU.add).then_inc(r_lg, 1)

            def attn_a(s, u):
                v = (u + 1) % 2
                if fixed(s) and s == 0:
                    dve.wait_ge(s_x0, 16)
                if fixed(s) and s == 2:
                    dve.wait_ge(s_x1, 16)
                b = s - 4
                if has(b):
                    dve.wait_ge(a_out_ps, b + 1)
                    dve.wait_ge(a_rinv, b + 1)
                    for i in range(TPB):
                        last = nc.vector.scalar_tensor_tensor(
                            out=X[:, ds(TPB * b + i), :], in0=PS[:, 6, i * D:(i + 1) * D], scalar=ria[:, u, i:i + 1],
                            in1=X[:, ds(TPB * b + i), :], op0=ALU.mult, op1=ALU.add)
                    last.then_inc(a_x, 1)
                if has(s):
                    if not fixed(s) or s >= 2:
                        dve.wait_ge(a_xT_ps, s - 1)
                    norm_stats(LN["A"], s, TPB * s, u)
                if has(b):
                    dve.wait_ge(a_x, b + 1)
                    wait(dve, r_tok, b - 1)
                    norm_stats(LN["F"], b, TPB * b, u)
                b = s - 3
                if has(b):
                    dve.wait_ge(a_exp, b + 1)
                    nc.vector.reciprocal(ria[:, v, :], rsa[:, v, :]).then_inc(a_rinv, 1)
                if has(s):
                    norm_apply(LN["A"], s, TPB * s, u)
                b = s - 4
                if has(b):
                    norm_apply(LN["F"], b, TPB * b, u)
                b = s - 1
                if has(b):
                    dve.wait_ge(a_qk_ps, b + 1)
                    if fixed(b) and b == 0:
                        dve.wait_ge(s_wa, 48)
                    wait(dve, a_rope, b)
                    nc.vector.tensor_tensor(rot[:, 0, :], PS[:, 0, :], ROPE[:, 0, :], ALU.mult).then_inc(a_rot, 1)
                b = s - 2
                if has(b):
                    dve.wait_ge(a_scores, b + 1)
                    wait(dve, a_exp, b - 1)
                    nc.vector.reduce_max(mxa[:, u, :], PS[:, 2, :].rearrange("p (t m) -> p t m", t=TPB),
                                         AX.X).then_inc(a_max, 1)
                    dve.wait_ge(a_max, b + 1)
                    nc.vector.tensor_scalar(nba[:, u, :], mxa[:, u, :], -SCALE_A, None, ALU.mult).then_inc(a_nb, 1)
                b = s - 1
                if has(b):
                    dve.wait_ge(a_rot, b + 1)
                    dve.wait_ge(a_sin, b + 1)
                    wait(dve, a_scores, b - 1)
                    nc.vector.tensor_tensor(qk[:, v, :, :].rearrange("p a m -> p (a m)"), rot[:, 0, :], rot[:, 1, :],
                                            ALU.add).then_inc(a_rope, 1)
                b = s - 5
                if has(b):
                    if fixed(b) and b == 0:
                        dve.wait_ge(s_wr, 32)
                    logits(b, TPB * b, 7)

            def route(k):
                g = k % GROUPS
                t0 = g * GT
                lg = LG[:, t0:t0 + GT, :]
                done = [STEPS * k]

                def then(ins):
                    done[0] += 1
                    ins.then_inc(r_step, 1)
                    dve.wait_ge(r_step, done[0])

                def over_e(ap):
                    return ap.unsqueeze(2).to_broadcast([P, GT, E])

                dve.wait_ge(r_lg, GB * (k + 1))
                then(nc.vector.reduce_max(r_mx[:, :], lg, AX.X))
                then(nc.vector.tensor_tensor(r_sh[:, :, :], lg, over_e(r_mx[:, :]), ALU.subtract))
                then(nc.vector.tensor_tensor(r_eq[:, :, :], lg, over_e(r_mx[:, :]), ALU.is_equal))
                e8 = CST[:, C_E8:C_E8 + E]
                then(nc.vector.tensor_tensor(r_eq[:, :, :], r_eq[:, :, :], e8[:, None, :].to_broadcast([P, GT, E]),
                                             ALU.mult))
                then(nc.vector.reduce_max(r_best[:, :], r_eq[:, :, :], AX.X))
                then(nc.vector.tensor_tensor(r_hot[:, :, :].rearrange("p e t -> p t e"),
                                             e8[:, None, :].to_broadcast([P, GT, E]), over_e(r_best[:, :]),
                                             ALU.is_equal))
                dve.wait_ge(r_exp, k + 1)
                then(nc.vector.reduce_sum(r_den[:, :], r_ex[:, :, :], AX.X))
                then(nc.vector.reciprocal(GATE[:, t0:t0 + GT], r_den[:, :]))
                dve.wait_ge(r_pre_ps, k + 1)
                then(nc.vector.tensor_copy(r_ps[:, :], PS[:, 7 if k < GROUPS else 6, 0:2 * E * GT]))
                assert done[0] == STEPS * k + READ_STEP
                pre = r_ps[:, 0:E * GT].rearrange("p (e t) -> p e t", e=E)
                tot = r_ps[:, E * GT:2 * E * GT]
                then(nc.vector.tensor_tensor_scan(r_inc[:, :, :].rearrange("p e t -> p (e t)"),
                                                  CST[:, C_SCAN:C_SCAN + E * GT], tot, 0.0, ALU.mult, ALU.add))
                then(nc.vector.tensor_tensor(r_exc[:, :, :].rearrange("p e t -> p (e t)"),
                                             r_inc[:, :, :].rearrange("p e t -> p (e t)"), tot, ALU.subtract))
                then(nc.vector.tensor_scalar(r_cnt[:, :], r_inc[:, :, GT - 1], float(P - 1), None, ALU.add))
                then(nc.vector.tensor_scalar(r_cnts[:, :], r_cnt[:, :], 7, None, ALU.logical_shift_right))
                then(nc.vector.tensor_copy(r_nt[:, :], r_cnts[:, :]))
                then(nc.vector.tensor_tensor_scan(r_cum[:, :], CST[:, C_ONE:C_ONE + E], r_nt[:, :], 0.0,
                                                  ALU.mult, ALU.add))
                then(nc.vector.tensor_tensor(r_base[:, :], r_cum[:, :], r_nt[:, :], ALU.subtract))
                then(nc.vector.scalar_tensor_tensor(
                    out=r_exc[:, :, :], in0=r_base[:, :].unsqueeze(2).to_broadcast([P, E, GT]), scalar=float(P),
                    in1=r_exc[:, :, :], op0=ALU.mult, op1=ALU.add))
                then(nc.vector.tensor_tensor(r_exc[:, :, :], pre, r_exc[:, :, :], ALU.add))
                then(nc.vector.tensor_tensor(r_exc[:, :, :], r_exc[:, :, :], r_hot[:, :, :], ALU.mult))
                then(nc.vector.reduce_sum(r_pos[:, :], r_exc[:, :, :].rearrange("p e t -> p t e"), AX.X))
                then(nc.vector.tensor_copy(r_posi[:, :], r_pos[:, :]))
                then(nc.vector.tensor_scalar(r_tile[:, :], r_posi[:, :], 7, None, ALU.logical_shift_right))
                then(nc.vector.tensor_copy(r_tilef[:, :], r_tile[:, :]))
                then(nc.vector.tensor_scalar(r_pos[:, :], r_pos[:, :], float(NJ), None, ALU.mult))
                then(nc.vector.scalar_tensor_tensor(out=POS[:, t0:t0 + GT], in0=r_tilef[:, :],
                                                    scalar=float(1 - NJ * P), in1=r_pos[:, :], op0=ALU.mult,
                                                    op1=ALU.add))
                then(nc.vector.tensor_tensor(
                    r_cmp[:, :, :], CST[:, C_TILE:C_TILE + NJ * E].rearrange("p (j e) -> p j e", e=E),
                    r_cum[:, None, :].to_broadcast([P, NJ, E]), ALU.is_ge))
                then(nc.vector.reduce_sum(r_te[:, :], r_cmp[:, :, :], AX.X))
                then(nc.vector.tensor_scalar(TE[:, g * NJ:(g + 1) * NJ], r_te[:, :], float(E - 1), None, ALU.min))
                assert done[0] == STEPS * (k + 1), done[0]

            def experts(layer):
                n0 = NL * layer

                def ring(j):
                    return n0 if fixed(j) and j < 2 else n0 + (j - 1)

                def step(s, u):
                    v, w, r = (u + 1) % 2, u % 2, u % RING
                    if has(s - 2, NL):
                        e = dve.value_load(TE[0:1, ds(s - 2)], min_val=0, max_val=E - 1)
                    j = s - 5
                    if has(j, NL):
                        n = n0 + j
                        dve.wait_ge(f_y_ps, n + 1)
                        nc.vector.tensor_tensor(XY[:, ds(j), :], PS[:, 4 + v, 0:D],
                                                w2b2[:, (u - 5) % RING, FC * D:W2W], ALU.add).then_inc(f_y, 1)
                    j = s - 2
                    if has(j, NL):
                        n = n0 + j
                        if fixed(j) and j == 0 and layer == 0:
                            dve.wait_ge(s_w1, 32)
                            dve.wait_ge(s_w2, 16 * (FC + 1))
                            dve.wait_ge(b_qk_ps, 4)
                        wait(dve, f_h_ps, ring(j))
                        wait(dve, f_gelu, ring(j))
                        nc.vector.tensor_copy(w1b1[:, w, :], W1S[:, ds(e), :])
                        wait(dve, f_y, n0 if fixed(j) and j < RING else n0 + (j - (RING - 1)))
                        nc.vector.tensor_copy(w2b2[:, (u - 2) % RING, :], W2S[:, ds(e), :]).then_inc(f_w, 1)
                    j = s
                    if has(j, NL):
                        for kk in range(GROUPS):
                            for c, (j0, _) in enumerate(XCHUNKS):
                                if fixed(j) and j == (kk * NJ if kk else j0):
                                    dve.wait_ge(xs_in[GROUPS * layer + kk][c], 16)
                        wait(dve, f_xT_ps, ring(j))
                        nc.vector.tensor_copy(xs1[:, w, :], XY[:, ds(j), :]).then_inc(f_in, 1)

                expert_steps(dve, step)

            def combine(tile, s_inc):
                for i in range(TPB):
                    last = nc.vector.scalar_tensor_tensor(
                        out=X[:, ds(tile + i), :], in0=TOK[:, ds(tile + i), :], scalar=GATE[:, ds(tile + i)],
                        in1=X[:, ds(tile + i), :], op0=ALU.mult, op1=ALU.add)
                if s_inc is not None:
                    last.then_inc(s_inc, 1)

            def attn_b(s, u):
                hb, fb, v = s - 1, s - 2, (u + 1) % 2
                for h in range(H):
                    if h % 2 == 0:
                        b, hh = (hb, h - 5) if h >= 5 else (fb, h - 5 + H)
                        if has(b):
                            pair = hh // 2
                            dve.wait_ge(b_av, b * H + (hh + 1))
                            if pair == 0:
                                wait(dve, b_out_ps, b - 1)
                            nc.vector.tensor_copy(yT[:, v if b is hb else u, pair, :],
                                                  PS[:, 7, 0:M]).then_inc(b_y, 1)
                    b, hh = (hb, h - 2) if h >= 2 else (fb, h - 2 + H)
                    if has(b):
                        cnt = b * H + hh
                        dve.wait_ge(b_exp, cnt + 1)
                        wait(dve, b_p, cnt - 3)
                        nc.vector.reciprocal(rib[:, hh % 4, :], rsb[:, hh % 4, :]).then_inc(b_rinv, 1)
                    b, hh = (hb, h - 1) if h >= 1 else (fb, H - 1)
                    if has(b):
                        cnt = b * H + hh
                        dve.wait_ge(b_s_ps, cnt + 1)
                        dve.sem_inc(dve_waited)
                        for c0, c1, m in ((0, P, C_MASK), (P, 3 * P, C_ZERO)):
                            ps = PS[:, hh % 2, c0:c1]
                            last = nc.vector.tensor_tensor_reduce(
                                ps, ps, CST[:, m:m + c1 - c0], 1.0, LOWEST, ALU.add, ALU.max,
                                mxb[:, hh % 4, c0 // P:c0 // P + 1])
                        last.then_inc(b_max, 1)
                        dve.wait_ge(b_max, cnt + 1)
                        nc.vector.tensor_scalar(nbb[:, hh % 4, :], mxb[:, hh % 4, :], -SCALE_B, None,
                                                ALU.mult).then_inc(b_nb, 1)
                    b, hh = (hb, h - 3) if h >= 3 else (fb, h - 3 + H)
                    if has(b):
                        cnt = b * H + hh
                        dve.wait_ge(b_pT_ps, cnt + 1)
                        wait(dve, b_av, cnt - 1)
                        nc.vector.tensor_copy(pTb[:, hh % 2, :], PS[:, 2 + hh % 2, 0:3 * P]).then_inc(b_pT, 1)
                    if h == 8 and has(fb):
                        dve.wait_ge(b_out_ps, fb + 1)
                        nc.vector.tensor_tensor(X[:, ds(TPB * fb, TPB), :],
                                                PS[:, 6, 0:TPB * D].rearrange("p (t d) -> p t d", t=TPB),
                                                X[:, ds(TPB * fb, TPB), :], ALU.add).then_inc(b_x, 1)
                        dve.wait_ge(b_x, fb + 1)
                        dve.wait_ge(r_tok, fb + (NB - 1))
                        norm_stats(LN["F"], fb + NB, TPB * fb, u)
                    if h == 9 and has(fb):
                        norm_apply(LN["F"], fb + NB, TPB * fb, u)
                    if h == 10 and has(s):
                        if fixed(s) and s in (0, GB):
                            dve.wait_ge(gathered[s // GB], 16 * GT)
                        combine(TPB * s, b_comb)
                        dve.wait_ge(b_comb, s + 1)
                        wait(dve, b_xT_ps, s - 1)
                        norm_stats(LN["B"], s, TPB * s, u)
                    if h == 12 and has(s):
                        norm_apply(LN["B"], s, TPB * s, u)
                    if h == 12 and has(fb):
                        logits(fb + NB, TPB * fb, 6)
                    if h == 14 and has(s):
                        dve.wait_ge(b_xT, s + 1)
                        nc.vector.tensor_tensor(one_pass(xl[:, u, :]), PS[:, 6, 0:M], xh[:, u, :],
                                                ALU.subtract).then_inc(b_xl, 1)

            peeled(attn_a, 0, 8)
            turns(dve, attn_a, 8, 14)
            route(0)
            turns(dve, attn_a, 14, 16)
            peeled(attn_a, 16, NB + 5)
            route(1)
            for q in range(4):
                dve.wait_ge(b_qk, q + 1)
                nc.vector.tensor_tensor(one_pass(QKl[:, 4 * q:4 * q + 4, :]),
                                        PS[:, q, :].rearrange("p (h d) -> p h d", h=4),
                                        QKh[:, 4 * q:4 * q + 4, :], ALU.subtract).then_inc(b_qkl, 1)
            dve.wait_ge(b_wv, 1)
            nc.vector.tensor_tensor(one_pass(WVBl[:, :]), WVB, WVBh[:, :], ALU.subtract).then_inc(b_qkl, 1)
            experts(0)
            peeled(attn_b, 0, 4)
            turns(dve, attn_b, 4, 8)
            peeled(attn_b, 8, 10)
            route(2)
            turns(dve, attn_b, 10, 16)
            peeled(attn_b, 16, 18)
            route(3)
            experts(1)
            dve.wait_ge(gathered[2], 16 * GT)
            for q in range(8):
                if q >= 4:
                    dve.wait_ge(last_gathered[q - 4], 64)
                for b in range(2):
                    combine(4 * q + TPB * b, x_done if b == 1 else None)

        @block.tensor
        def _(pe):
            mm, tr = nc.tensor.matmul, nc.tensor.transpose

            def split(ps, lhs, rhs):
                mm(ps, one_pass(lhs[0]), one_pass(rhs[0]), start=True, stop=False)
                mm(ps, one_pass(lhs[0]), one_pass(rhs[1]), start=False, stop=False)
                return mm(ps, one_pass(lhs[1]), one_pass(rhs[0]), start=False, stop=True)

            def router_T(n, slot, bank):
                pe.wait_ge(LN["F"]["s_out"], n + 1)
                for i in range(TPB):
                    last = tr(PS[:, bank, i * P:(i + 1) * P], LN["F"]["out"][:, slot, i, :], ident)
                last.then_inc(r_xT_ps, 1)

            def router(n, slot, bank):
                pe.wait_ge(r_xT, n + 1)
                for i in range(TPB):
                    last = mm(PS[:, bank, M + i * E:M + (i + 1) * E], fT[:, slot, i * P:(i + 1) * P], WRS[:, :],
                              start=True, stop=True)
                last.then_inc(r_lg_ps, 1)

            def attn_a(s, u):
                v = (u + 1) % 2
                b = s - 1
                if has(b):
                    pe.wait_ge(LN["A"]["s_out"], b + 1)
                    wait(pe, a_xT, b)
                    for i in range(TPB):
                        last = tr(PS[:, 4, i * P:(i + 1) * P], LN["A"]["out"][:, v, i, :], ident)
                    last.then_inc(a_xT_ps, 1)
                b = s - 5
                if has(b):
                    if fixed(b) and b == 0:
                        pe.wait_ge(s_wr, 32)
                    wait(pe, r_lg, b)
                    router_T(b, v, 7)
                b = s - 3
                if has(b):
                    pe.wait_ge(a_exp, b + 1)
                    wait(pe, a_pT, b)
                    for kc in range(TPB):
                        for i in range(TPB):
                            last = tr(PS[:, 3, kc * M + i * P:kc * M + (i + 1) * P],
                                      pa[:, v, i, kc * P:(kc + 1) * P], ident)
                    last.then_inc(a_pT_ps, 1)
                b = s - 1
                if has(b):
                    if fixed(b) and b == 0:
                        pe.wait_ge(s_wa, 48)
                    pe.wait_ge(a_xT, b + 1)
                    wait(pe, a_rot, b)
                    wait(pe, a_qks, b)
                    for i in range(2):
                        for w in range(2):
                            last = mm(PS[:, i, w * M:(w + 1) * M], WQK[:, 2 * w + i, :], xnT[:, v, :],
                                      start=True, stop=True)
                    last.then_inc(a_qk_ps, 1)
                b = s - 2
                if has(b):
                    pe.wait_ge(a_rope, b + 1)
                    wait(pe, a_exp, b)
                    for i in range(TPB):
                        last = mm(PS[:, 2, i * M:(i + 1) * M], qk[:, u, 0, i * P:(i + 1) * P], qk[:, u, 1, :],
                                  start=True, stop=True)
                    last.then_inc(a_scores, 1)
                b = s - 1
                if has(b):
                    wait(pe, a_v, b)
                    for i in range(TPB):
                        last = mm(PS[:, 5, i * D:(i + 1) * D], xnT[:, v, i * P:(i + 1) * P], WVA[:, :],
                                  start=True, stop=True)
                    last.then_inc(a_v_ps, 1)
                b = s - 3
                if has(b):
                    pe.wait_ge(a_pT, b + 1)
                    pe.wait_ge(a_v, b + 1)
                    wait(pe, a_x, b)
                    for i in range(TPB):
                        for kc in range(TPB):
                            last = mm(PS[:, 6, i * D:(i + 1) * D], pTa[:, v, kc, i * P:(i + 1) * P],
                                      va[:, v, kc, :], start=kc == 0, stop=kc == TPB - 1)
                    last.then_inc(a_out_ps, 1)
                b = s - 5
                if has(b):
                    router(b, v, 7)

            def route(k):
                pe.wait_ge(r_step, STEPS * k + HOT_STEP)
                bank = 7 if k < GROUPS else 6
                if k >= GROUPS:
                    pe.wait_ge(b_xl, 10 if k == 2 else NB)
                hot = r_hot[:, :, :].rearrange("p e t -> p (e t)")
                mm(PS[:, bank, 0:E * GT], upperb[:, :], hot, start=True, stop=True)
                mm(PS[:, bank, E * GT:2 * E * GT], onesb[:, :], hot, start=True, stop=True).then_inc(r_pre_ps, 1)
                pe.wait_ge(r_step, STEPS * k + READ_STEP)

            def experts(layer):
                n0 = NL * layer

                def ring(j):
                    return n0 if fixed(j) and j < 2 else n0 + (j - 1)

                def step(s, u):
                    v, w, r = (u + 1) % 2, u % 2, u % RING
                    j = s - 1
                    if has(j, NL):
                        n = n0 + j
                        pe.wait_ge(f_in, n + 1)
                        wait(pe, f_xT, ring(j))
                        tr(PS[:, 2 + v, 0:P], xs1[:, v, :], ident).then_inc(f_xT_ps, 1)
                    j = s - 3
                    if has(j, NL):
                        n = n0 + j
                        pe.wait_ge(f_xT, n + 1)
                        pe.wait_ge(f_w, n + 1)
                        wait(pe, f_gelu, ring(j))
                        for c in range(FC):
                            last = mm(PS[:, v, c * P:(c + 1) * P], w1b1[:, v, c * P:(c + 1) * P], xsT[:, v, :],
                                      start=True, stop=True)
                        last.then_inc(f_h_ps, 1)
                    j = s - 4
                    if has(j, NL):
                        n = n0 + j
                        pe.wait_ge(f_gelu, n + 1)
                        wait(pe, f_y, ring(j))
                        for c in range(FC):
                            last = mm(PS[:, 4 + w, 0:D], hT[:, w, c, :], w2b2[:, r, c * D:(c + 1) * D],
                                      start=c == 0, stop=c == FC - 1)
                        last.then_inc(f_y_ps, 1)

                expert_steps(pe, step)

            def attn_b(s, u):
                hb, fb, v = s - 1, s - 2, (u + 1) % 2

                def scores(b, hh, slot):
                    cnt = b * H + hh
                    pe.wait_ge(b_g, cnt + 1)
                    wait(pe, b_exp, cnt - 1)
                    ps = PS[:, hh % 2, :]
                    mm(ps[:, 0:P], gT[:, hh % 2, 0:P], xnT[:, slot, 0:P], start=True, stop=True)
                    mm(ps[:, P:3 * P], gT[:, hh % 2, P:M], xnT[:, slot, :], start=True, stop=True).then_inc(b_s_ps, 1)

                def transposes(b, hh):
                    cnt = b * H + hh
                    pe.wait_ge(b_p, cnt + 1)
                    wait(pe, b_pT, cnt - 1)
                    for c in range(3):
                        last = tr(PS[:, 2 + hh % 2, c * P:(c + 1) * P], pb[:, hh % 4, c * P:(c + 1) * P], ident)
                    last.then_inc(b_pT_ps, 1)

                def product(b, hh, slot):
                    cnt = b * H + hh
                    pe.wait_ge(b_pT, cnt + 1)
                    if hh == 0:
                        pe.wait_ge(b_v, b * 4 + 4)
                    if hh % 2 == 0:
                        wait(pe, b_y, b * NPAIR + hh // 2)
                    q = DK * (hh % 2)
                    mm(PS[q:q + DK, 7, 0:M], vb[:, slot, 0, hh * DK:(hh + 1) * DK], pTb[:, hh % 2, 0:M],
                       start=True, stop=True)
                    last = mm(PS[q:q + DK, 7, P:M], vb[:, slot, 1, hh * DK:(hh + 1) * DK], pTb[:, hh % 2, M:3 * P],
                              start=False, stop=True, skip_group_check=True)
                    last.then_inc(b_av, 1)

                for h in range(H):
                    if has(hb):
                        cnt = hb * H + h
                        if h == 0:
                            pe.wait_ge(b_xT, hb + 1)
                            pe.wait_ge(b_xl, hb + 1)
                        wait(pe, b_g, cnt - 1)
                        split(PS[:, 4 + h % 2, 0:M], (QKh[:, h, :], QKl[:, h, :]), (xh[:, v, :], xl[:, v, :])
                              ).then_inc(b_g_ps, 1)
                        if h < 4:
                            if h > 0:
                                pe.wait_ge(b_v, hb * 4 + h)
                            i, c = h % 2, h // 2
                            split(PS[:, 6, :], [x_[:, v, i * P:(i + 1) * P] for x_ in (xh, xl)],
                                  [w_[:, c * 512:(c + 1) * 512] for w_ in (WVBh, WVBl)]).then_inc(b_v_ps, 1)
                    if h >= 1 and has(hb):
                        scores(hb, h - 1, v)
                    if h == 0 and has(fb):
                        scores(fb, H - 1, u)
                    if h >= 3 and has(hb):
                        transposes(hb, h - 3)
                    if h < 3 and has(fb):
                        transposes(fb, h - 3 + H)
                    if h >= 4 and has(hb):
                        product(hb, h - 4, v)
                    if h < 4 and has(fb):
                        product(fb, h - 4 + H, u)
                    if h in (6, 7) and has(fb):
                        i = h - 6
                        if i == 0:
                            pe.wait_ge(b_y, fb * NPAIR + NPAIR)
                            if has(hb):
                                pe.wait_ge(b_v, hb * 4 + 4)
                        for pair in range(NPAIR):
                            last = mm(PS[:, 6, i * D:(i + 1) * D], yT[:, u, pair, i * P:(i + 1) * P], WO[:, pair, :],
                                      start=pair == 0, stop=pair == NPAIR - 1)
                        if i == 1:
                            last.then_inc(b_out_ps, 1)
                    if h == 10 and has(fb):
                        router_T(fb + NB, u, 6)
                    if h == 11 and has(fb):
                        router(fb + NB, u, 6)
                    if h == 13 and has(s):
                        pe.wait_ge(LN["B"]["s_out"], s + 1)
                        if has(fb):
                            pe.wait_ge(r_lg, fb + (NB + 1))
                        elif has(hb):
                            pe.wait_ge(b_v, hb * 4 + 4)
                        for i in range(TPB):
                            last = tr(PS[:, 6, i * P:(i + 1) * P], LN["B"]["out"][:, u, i, :], ident)
                        last.then_inc(b_xT_ps, 1)

            pe.wait_ge(s_cst, 16)
            pe.wait_ge(s_castb, 1)
            peeled(attn_a, 0, 8)
            turns(pe, attn_a, 8, 14)
            route(0)
            turns(pe, attn_a, 14, 16)
            peeled(attn_a, 16, NB + 5)
            route(1)
            pe.wait_ge(s_wb, 64)
            for h in range(H):
                last = mm(PS[:, h // 4, (h % 4) * P:(h % 4 + 1) * P], WQB[:, h, :], WKB[:, h, :],
                          start=True, stop=True)
                if h % 4 == 3:
                    last.then_inc(b_qk_ps, 1)
            pe.wait_ge(b_qkl, 5)
            experts(0)
            pe.wait_ge(f_y, 2 * NJ)
            peeled(attn_b, 0, 4)
            turns(pe, attn_b, 4, 10)
            route(2)
            turns(pe, attn_b, 10, 16)
            peeled(attn_b, 16, 18)
            route(3)
            experts(1)


STEPS, SHIFT_STEP, HOT_STEP, READ_STEP = 28, 2, 6, 9

_OUT = (NB, M, D)


def tables():
    i = np.arange(D // 2, dtype=np.float32)
    theta = np.power(np.float32(10000.0), (np.float32(-2.0) * (i - np.float32(1.0)) / np.float32(D)).astype(np.float32))
    ang = (np.arange(M, dtype=np.float32)[:, None] * theta[None, :].astype(np.float32)).astype(np.float32)
    cos, sin = np.cos(ang).T, np.sin(ang).T
    rope = np.zeros((P, 2, 2, M), np.float32)
    rope[0::2, 0], rope[1::2, 0] = cos[:, None, :], cos[:, None, :]
    rope[0::2, 1], rope[1::2, 1] = sin[:, None, :], -sin[:, None, :]
    cst = np.zeros((P, C_W), np.float32)
    r = np.arange(P)
    cst[:, C_ID:C_ID + P] = np.eye(P)
    cst[:, C_UP:C_UP + P] = r[:, None] < r[None, :]
    cst[:, C_ONE:C_ONE + P] = 1.0
    cst[:, C_ZERO:C_ZERO + P] = 0.0
    cst[:, C_MASK:C_MASK + P] = np.where(r[:, None] < r[None, :], MASKED, 0.0)
    cst[:, C_E8:C_E8 + E] = E - np.arange(E)
    cst[:, C_SCAN:C_SCAN + E * GT] = (np.arange(E * GT) % GT != 0)
    cst[:, C_TILE:C_TILE + NJ * E] = np.arange(NJ * E) // E
    return rope.reshape(P, 2, 2 * M), cst


def kernel(**inputs):
    import concourse.bacc as _bacc
    from concourse.bass_utils import run_bass_kernel_spmd as _run

    a = {n.replace("L0_", ""): np.asarray(v) for n, v in inputs.items()}
    swap = np.arange(D) ^ 1
    wq, wk = a["attn_a_wq"].T, a["attn_a_wk"].T
    rope, cst = tables()
    arrays = {
        "x": a["attn_a_x"],
        "wqk_a": np.stack([wq, wq[:, swap], wk, wk[:, swap]], axis=1),
        "wv_a": a["attn_a_wv"].T,
        "rope": rope,
        "w_q": a["attn_b_w_q"],
        "w_k": a["attn_b_w_k"],
        "wv_b": a["attn_b_w_v"].reshape(H * DK, D).T,
        "w_o": a["attn_b_w_o"],
        "W1": a["ffn_W1"],
        "b1t": a["ffn_b1"].reshape(E, FC, P).transpose(2, 0, 1),
        "W2": a["ffn_W2"],
        "b2": a["ffn_b2"],
        "Wr": a["ffn_Wr"],
        "br": a["ffn_br"],
        "cst": cst,
    }
    arrays = {f"in_{n}": np.ascontiguousarray(v) for n, v in arrays.items()}
    nc = _bacc.Bacc("TRN2", target_bir_lowering=False, num_devices=1)
    args = [nc.dram_tensor(n, v.shape, mybir.dt.from_np(v.dtype), kind="ExternalInput").ap()
            for n, v in arrays.items()]
    out = nc.dram_tensor("out_dram", _OUT, F32, kind="ExternalOutput").ap()
    build(nc, *args, out)
    r = _run(nc, [arrays], core_ids=[0])
    return r.results[0]["out_dram"]
```

```python
from contextlib import ExitStack

import numpy as np
import concourse.bass as bass
from concourse import mybir

F32 = mybir.dt.float32
F32R = mybir.dt.float32r
BF16 = mybir.dt.bfloat16
I32 = mybir.dt.int32
ALU = mybir.AluOpType
ACT = mybir.ActivationFunctionType
AX = mybir.AxisListType

P = 128
NB, M, D = 16, 256, 128
TPB = M // P
NT = NB * TPB
H, DK = 16, 64
NPAIR = H // 2
E, F = 8, 512
FC = F // P
GROUPS = 2
GB = NB // GROUPS
GT = GB * TPB
NJ = GT + E - 1
NL = GROUPS * NJ
DI = D + 1
NONE = GT * P
W1W = F + FC
W2W = FC * D + D
RING = 4
EPS = 1e-5
SCALE_A = float(1.0 / np.sqrt(np.float32(D)))
SCALE_B = float(1.0 / np.sqrt(np.float32(DK)))
MASKED, HIGHEST = -3.0e38, 3.4e38
LENT = 20
XCHUNKS = ((0, 4), (4, NJ))

C_ID, C_UP, C_ONE = 0, P, 2 * P
C_ZERO, C_MASK = 3 * P, 4 * P
C_E8 = 5 * P
C_SCAN = C_E8 + E
C_TILE = C_SCAN + E * GT
C_W = C_TILE + NJ * E


def one_pass(ap):
    return ap.bitcast(F32R)


def ds(i, n=1):
    return bass.ds(i, n)


def fixed(v):
    return isinstance(v, int)


def wait(eng, sem, value):
    if not fixed(value) or value > 0:
        eng.wait_ge(sem, value)


def turns(eng, body, first, last, n=2):
    assert first % n == 0 and last % n == 0
    with eng.Fori(first // n, last // n) as turn:
        for u in range(n):
            body(turn * n + u, u)


def peeled(body, first, last, n=2):
    for s in range(first, last):
        body(s, s % n)


def head_at(h):
    return h ^ 1


VT, VW = 8, M


def expert_steps(eng, step, first=0, beside=None):
    second, tail = NJ // RING * RING, NL // RING * RING
    peeled(step, first, 2 * RING, RING)
    turns(eng, step, 2 * RING, second, RING)
    peeled(step, second, second + RING, RING)
    turns(eng, step, second + RING, tail, RING)
    for s in range(tail, NL + 5):
        step(s, s % RING)
        if beside is not None and NL <= s < NL + 4:
            beside(s - NL)


def has(b, n=NB):
    return not fixed(b) or 0 <= b < n


def build(nc, ids, x, wqk_a, wv_a, rope, w_q, w_k, wv_b, w_o, W1, b1t, W2, b2, Wr, br, cst, out):
    ctx = ExitStack()
    with ctx:
        def sb(name, shape, dt=F32):
            return ctx.enter_context(nc.sbuf_tensor(name, shape, dt))

        def sem(name):
            return ctx.enter_context(nc.semaphore(name))

        xs_dram = [nc.dram_tensor(f"xs_dram{k}", [P * NJ, DI], F32, kind="Internal").ap() for k in range(4)]
        yt_dram = [nc.dram_tensor(f"yt_dram{k}", [NONE + P * NJ, D], F32, kind="Internal").ap() for k in range(4)]

        X = sb("X", [P, NT, D])
        CST = sb("CST", [P, C_W])
        ident = CST[:, C_ID:C_ID + P]
        upperb = sb("upperb", [P, P], BF16)
        onesb = sb("onesb", [P, P], BF16)
        half = sb("half", [P, TPB])
        WQK = sb("WQK", [P, 4, D])
        WVA = sb("WVA", [P, D])
        ROPE = sb("ROPE", [P, 2, 2 * M])
        QKh, QKl = (sb(n, [P, H, D]) for n in ("QKh", "QKl"))
        WVBh, WVBl = (sb(n, [P, H * DK]) for n in ("WVBh", "WVBl"))
        WO = sb("WO", [P, NPAIR, D])
        W1S = sb("W1S", [P, E, W1W])
        W2S = sb("W2S", [P, E, W2W])
        WRS = sb("WRS", [P, E])
        BRS = sb("BRS", [P, E])
        LN = {}
        for n in "AFB":
            LN[n] = {
                "stats": sb(f"stats{n}", [P, 2, TPB, 6]), "mv": sb(f"mv{n}", [P, 2, TPB, 2]),
                "var": sb(f"var{n}", [P, 2, TPB]), "rstd": sb(f"rstd{n}", [P, 2, TPB]),
                "out": LN["A"]["out"] if n == "B" else sb(f"ln{n}", [P, 2, TPB, D]),
                "s_stats": sem(f"ln{n}_stats"), "s_mv": sem(f"ln{n}_mv"), "s_var": sem(f"ln{n}_var"),
                "s_rstd": sem(f"ln{n}_rstd"), "s_out": sem(f"ln{n}_out"),
            }
        TOK = sb("TOK", [P, NT, DI])
        XY = sb("XY", [P, NL, DI])
        lent = XY[:, NJ:NL, :].rearrange("p j d -> p (j d)")
        xs1 = sb("xs1", [P, 2, D])
        w1b1 = sb("w1b1", [P, 2, W1W])
        xnT = sb("xnT", [P, 2, M])
        rot = w1b1[:, :, 0:2 * M]
        qks = lent[:, 4 * TPB * M:4 * TPB * M + 2 * M]
        qk = sb("qk", [P, 2, 2, M])
        va = sb("va", [P, 2, TPB, D])
        mxa, nba, rsa, ria = (sb(n, [P, 2, TPB]) for n in ("mxa", "nba", "rsa", "ria"))
        pa = lent[:, 0:2 * TPB * M].rearrange("p (a b m) -> p a b m", a=2, b=TPB)
        pTa = lent[:, 2 * TPB * M:4 * TPB * M].rearrange("p (a b m) -> p a b m", a=2, b=TPB)
        xh, xl = (sb(n, [P, 2, M]) for n in ("xh", "xl"))
        g0 = lent[:, 2 * H * DK:2 * H * DK + 2 * P].rearrange("p (a q) -> p a q", a=2)
        gh, gl = (sb(n, [P, 2, P]) for n in ("gh", "gl"))
        nbb, rsb, rib = (sb(n, [P, 4, TPB]) for n in ("nbb", "rsb", "rib"))
        pb = sb("pb", [P, 4, 3 * P])
        pTh, pTl = (sb(n, [P, 2, M]) for n in ("pTh", "pTl"))
        pT1 = lent[:, 2 * H * DK + 2 * P:2 * H * DK + 4 * P].rearrange("p (a q) -> p a q", a=2)
        vh, vl = (sb(n, [P, 2, H * DK]) for n in ("vh", "vl"))
        v1 = lent[:, 0:2 * H * DK].rearrange("p (a c) -> p a c", a=2)
        yT = sb("yT", [P, 2, NPAIR, M])
        WQB = yT[0:DK, 0, :, :].rearrange("p a (c d) -> p (a c) d", c=2)
        WKB = yT[0:DK, 1, :, :].rearrange("p a (c d) -> p (a c) d", c=2)
        WVB = pb.rearrange("p a b -> p (a b)")[:, 0:H * DK]
        yflat = yT.rearrange("p a b m -> p (a b m)")
        w2b2 = yflat[:, 0:RING * W2W].rearrange("p (r w) -> p r w", r=RING)
        hT = yflat[:, RING * W2W:RING * W2W + 2 * F].rearrange("p (a c t) -> p a c t", a=2, c=FC)
        fT = sb("fT", [P, 2, M])
        LG = sb("LG", [P, NT, E])
        GATE = sb("GATE", [P, NT])
        IDS = sb("IDS", [P, NT + NJ], I32)
        POS = sb("POS", [P, NT], I32)
        TE = sb("TE", [P, NL], I32)
        r_mx = sb("r_mx", [P, GT])
        r_sh = sb("r_sh", [P, GT, E])
        r_ex = sb("r_ex", [P, GT, E])
        r_den = sb("r_den", [P, GT])
        r_eq = sb("r_eq", [P, GT, E])
        r_best = sb("r_best", [P, GT])
        r_ps = sb("r_ps", [P, 2 * E * GT])
        r_hot = sb("r_hot", [P, E, GT], BF16)
        r_inc = sb("r_inc", [P, E, GT])
        r_exc = sb("r_exc", [P, E, GT])
        r_cnt = sb("r_cnt", [P, E], I32)
        r_cnts = sb("r_cnts", [P, E], I32)
        r_nt = sb("r_nt", [P, E])
        r_cum = sb("r_cum", [P, E])
        r_base = sb("r_base", [P, E])
        r_pos = sb("r_pos", [P, GT])
        r_posi = sb("r_posi", [P, GT], I32)
        r_tile = sb("r_tile", [P, GT], I32)
        r_tilef = sb("r_tilef", [P, GT])
        r_cmp = sb("r_cmp", [P, NJ, E])
        r_te = sb("r_te", [P, NJ])
        xsT = sb("xsT", [P, 2, P])
        PS = ctx.enter_context(nc.psum_tensor("PS", [P, 8, 512], F32))

        s_cst, s_x0, s_x1, s_wa, s_wb, s_wr, s_w1, s_w2, s_xs0 = (
            sem(n) for n in ("cst_in", "x_first_in", "x_rest_in", "w_attn_a_in", "w_attn_b_in", "w_router_in",
                             "w1_in", "w2_in", "xs_zeroed"))
        s_castb, s_zero = sem("consts_cast"), sem("zeros_set")
        (a_xT_ps, a_xT, a_qk_ps, a_qks, a_sin, a_rot, a_rope, a_v_ps, a_v, a_scores, a_max, a_nb, a_exp, a_rinv, a_pT_ps, a_pT,
         a_out_ps, a_x) = (sem("a_" + n) for n in (
             "xT_ps", "xT", "qk_ps", "qks", "sin", "rot", "rope", "v_ps", "v", "scores", "max", "nb", "exp", "rinv", "pT_ps", "pT",
             "out_ps", "x"))
        r_xT_ps, r_xT, r_tok, r_lg_ps, r_lg = (sem("r_" + n) for n in ("xT_ps", "xT", "tok", "lg_ps", "lg"))
        r_step, r_exp, r_pre_ps = (sem("r_" + n) for n in ("step", "exp", "pre_ps"))
        scattered = [sem(f"scattered{k}") for k in range(4)]
        gathered = [sem(f"gathered{k}") for k in range(4)]
        last_gathered = [sem(f"last_gathered{q}") for q in range(4)]
        s_ids = sem("numbers_in")
        xs_in = [[sem(f"xs_in{k}_{c}") for c in range(len(XCHUNKS))] for k in range(4)]
        returned, lent_returned = [sem(f"returned{k}") for k in range(4)], sem("lent_returned")
        f_in, f_xT_ps, f_xT, f_w, f_h_ps, f_gelu, f_y_ps, f_y = (
            sem("f_" + n) for n in ("in", "xT_ps", "xT", "w", "h_ps", "gelu", "y_ps", "y"))
        b_qk_ps, b_qk, b_qkl, b_wv = (sem(n) for n in ("b_qk_ps", "b_qk", "b_qkl", "b_wv"))
        b_comb, b_xT_ps, b_xT, b_xl, b_v_ps, b_v, b_vl, b_out_ps, b_x = (
            sem("b_" + n) for n in ("comb", "xT_ps", "xT", "xl", "v_ps", "v", "vl", "out_ps", "x"))
        b_g_ps, b_g, b_gl, b_s_ps, b_nb, b_exp, b_rinv, b_p, b_pT_ps, b_pTh, b_pT, b_av, b_y = (
            sem("b_h" + n) for n in ("g_ps", "g", "gl", "s_ps", "nb", "exp", "rinv", "p", "pT_ps", "pTh", "pT", "av", "y"))
        dve_waited, pool_waited = sem("dve_waited"), sem("pool_waited")
        x_done, s_out = sem("x_done"), sem("out_stored")

        block = ctx.enter_context(nc.Block())

        @block.sync
        def _(sp):
            xv = x.rearrange("b (t p) d -> p (b t) d", p=P)
            sp.dma_start(CST[:, :], cst).then_inc(s_cst, 16)
            sp.dma_start(IDS[:, :], ids).then_inc(s_ids, 16)
            sp.dma_start(X[:, 0:4, :], xv[:, 0:4, :]).then_inc(s_x0, 16)
            sp.dma_start(WQK[:, :, :], wqk_a).then_inc(s_wa, 16)
            sp.dma_start(ROPE[:, :, :], rope).then_inc(s_wa, 16)
            sp.dma_start(WVA[:, :], wv_a).then_inc(s_wa, 16)
            sp.dma_start(WRS[:, :], Wr).then_inc(s_wr, 16)
            sp.dma_start(BRS[:, :], br.rearrange("(a e) -> a e", a=1).to_broadcast([P, E])).then_inc(s_wr, 16)
            sp.dma_start(X[:, 4:NT, :], xv[:, 4:NT, :]).then_inc(s_x1, 16)
            sp.wait_ge(s_zero, 3)
            for k in range(4):
                sp.dma_start(xs_dram[k].rearrange("(p j) d -> p j d", p=P), XY[:, 0:NJ, :]).then_inc(s_xs0, 16)
            sp.dma_start(W1S[:, :, 0:F], W1.rearrange("e d f -> d e f")).then_inc(s_w1, 16)
            sp.dma_start(W1S[:, :, F:W1W], b1t).then_inc(s_w1, 16)
            for c in range(FC):
                sp.dma_start(W2S[:, :, c * D:(c + 1) * D],
                             W2[:, c * P:(c + 1) * P, :].rearrange("e p d -> p e d")).then_inc(s_w2, 16)
            sp.dma_start(W2S[:, :, FC * D:W2W], b2.rearrange("(a e) d -> a e d", a=1).to_broadcast([P, E, D])
                         ).then_inc(s_w2, 16)
            sp.dma_start(WQB, w_q.rearrange("h k c -> k h c")).then_inc(s_wb, 16)
            sp.dma_start(WKB, w_k.rearrange("h k c -> k h c")).then_inc(s_wb, 16)
            sp.dma_start(WVB, wv_b).then_inc(s_wb, 16)
            sp.dma_start(WO[:, :, :], w_o.rearrange("(a p) d -> p a d", p=P)).then_inc(s_wb, 16)
            for k in range(4):
                g = k % GROUPS
                xsv = xs_dram[k].rearrange("(p j) d -> p j d", p=P)
                sp.wait_ge(scattered[k], 16 * GT)
                for c, (j0, j1) in enumerate(XCHUNKS):
                    sp.dma_start(XY[:, g * NJ + j0:g * NJ + j1, :], xsv[:, j0:j1, :]).then_inc(xs_in[k][c], 16)
                if k % 2 == 1:
                    for kk in (k - 1, k):
                        sp.wait_ge(returned[kk], 16 * (NJ - LENT if kk == 1 else NJ))
                        if kk == 1:
                            sp.wait_ge(lent_returned, 16 * LENT)
                        ytv = yt_dram[kk][0:NONE, :].rearrange("(t p) d -> p t d", p=P)
                        t0 = GT * (kk % GROUPS)
                        for q in range(4) if kk == 3 else (0,):
                            a, b = (4 * q, 4 * q + 4) if kk == 3 else (0, GT)
                            sp.dma_start(TOK[:, t0 + a:t0 + b, 0:D], ytv[:, a:b, :]).then_inc(
                                last_gathered[q] if kk == 3 else gathered[kk], 16)
            ov = out.rearrange("b (t p) d -> p (b t) d", p=P)
            for q in range(8):
                sp.wait_ge(x_done, q + 1)
                sp.dma_start(ov[:, 4 * q:4 * q + 4, :], X[:, 4 * q:4 * q + 4, :]).then_inc(s_out, 16)
            sp.wait_ge(s_out, 8 * 16)

        @block.gpsimd
        def _(pool):
            nc.gpsimd.memset(XY[:, 0:NJ, 0:D], 0.0).then_inc(s_zero, 1)
            pool.wait_ge(s_ids, 16)
            nc.gpsimd.tensor_copy(XY[:, 0:NJ, D].bitcast(I32), IDS[:, NT:NT + NJ]).then_inc(s_zero, 1)
            nc.gpsimd.tensor_copy(TOK[:, :, D].bitcast(I32), IDS[:, 0:NT]).then_inc(s_zero, 1)
            pool.wait_ge(s_castb, 1)

            def rstd(ln, n, slot):
                pool.wait_ge(ln["s_var"], n + 1)
                nc.gpsimd.tensor_tensor(ln["rstd"][:, slot, :], ln["var"][:, slot, :], half[:, :],
                                        ALU.pow).then_inc(ln["s_rstd"], 1)

            def scatter(k, t):
                tile = GT * (k % GROUPS) + t
                nc.gpsimd.indirect_dma_start(
                    out=xs_dram[k], out_offset=bass.IndirectOffsetOnAxis(ap=POS[:, tile:tile + 1], axis=0),
                    in_=TOK[:, tile, :], in_offset=None).then_inc(scattered[k], 16)

            def before_scatters(k):
                pool.wait_ge(r_step, STEPS * (k + 1))
                pool.wait_ge(r_tok, GB * (k + 1))
                pool.wait_ge(s_xs0, 64)

            def give_back(k):
                for j in range(NJ):
                    if k == 1 and j == LENT:
                        attn_b(0, 0)
                    tile = NJ * (k % GROUPS) + j
                    pool.wait_ge(f_y, NJ * k + j + 1)
                    nc.gpsimd.indirect_dma_start(
                        out=yt_dram[k],
                        out_offset=bass.IndirectOffsetOnAxis(ap=XY[:, tile, D:DI].bitcast(I32), axis=0),
                        in_=XY[:, tile, 0:D], in_offset=None).then_inc(
                            lent_returned if k == 1 and j < LENT else returned[k], 16)

            def attn_a(s, u):
                if has(s):
                    rstd(LN["A"], s, u)
                if has(s - 4):
                    rstd(LN["F"], s - 4, u)
                b = s - 1
                if has(b):
                    pool.wait_ge(a_qks, b + 1)
                    wait(pool, a_rope, b)
                    if fixed(b) and b == 0:
                        pool.wait_ge(s_wa, 48)
                    nc.gpsimd.tensor_tensor(rot[:, 1, :], qks[:, :], ROPE[:, 1, :], ALU.mult).then_inc(a_sin, 1)

            peeled(attn_a, 0, 8)
            turns(pool, attn_a, 8, 14)
            for s in range(14, NB + 5):
                attn_a(s, s % 2)
                if s == 14:
                    before_scatters(0)
                for t in range(3 * (s - 14), min(3 * (s - 13), GT)):
                    scatter(0, t)
            before_scatters(1)
            for t in range(GT):
                scatter(1, t)

            def attn_b(s, u, more=None):
                hb, fb = s - 1, s - 2
                for h in range(H):
                    b, hh = (hb, h - 2) if h >= 2 else (fb, h - 2 + H)
                    if has(b):
                        pool.wait_ge(b_rinv, b * H + (hh + 1))
                        pool.sem_inc(pool_waited)
                        nc.gpsimd.tensor_scalar(pb[:, hh % 4, 0:P], pb[:, hh % 4, 0:P], rib[:, hh % 4, 0:1], 1.0,
                                                ALU.mult, ALU.mult)
                        nc.gpsimd.tensor_scalar(pb[:, hh % 4, P:3 * P], pb[:, hh % 4, P:3 * P], rib[:, hh % 4, 1:2],
                                                1.0, ALU.mult, ALU.mult).then_inc(b_p, 1)
                    if h == 12 and has(fb):
                        rstd(LN["F"], fb + NB, u)
                    if h == 6 and has(s):
                        rstd(LN["B"], s, u)
                    if more is not None:
                        more(h)

            def scatter2(h):
                if h == 0:
                    before_scatters(2)
                scatter(2, h)

            give_back(0)
            give_back(1)
            peeled(attn_b, 1, 4)
            turns(pool, attn_b, 4, 10)
            attn_b(10, 0)
            attn_b(11, 1, scatter2)
            turns(pool, attn_b, 12, 16)
            peeled(attn_b, 16, 18)
            before_scatters(3)
            for t in range(GT):
                scatter(3, t)
            give_back(2)
            give_back(3)

        @block.scalar
        def _(act):
            def router_copies(n, tile, slot, bank):
                act.wait_ge(LN["F"]["s_out"], n + 1)
                nc.scalar.copy(TOK[:, ds(tile, TPB), 0:D], LN["F"]["out"][:, slot, :, :]).then_inc(r_tok, 1)
                act.wait_ge(r_xT_ps, n + 1)
                wait(act, r_lg_ps, n - 1)
                nc.scalar.copy(fT[:, slot, :], PS[:, bank, 0:M]).then_inc(r_xT, 1)

            def attn_a(s, u):
                v = (u + 1) % 2
                b = s - 1
                if has(b):
                    act.wait_ge(a_xT_ps, b + 1)
                    wait(act, a_v_ps, b - 1)
                    nc.scalar.copy(xnT[:, v, :], PS[:, 4, 0:M]).then_inc(a_xT, 1)
                b = s - 5
                if has(b):
                    router_copies(b, TPB * b, v, 7)
                b = s - 3
                if has(b):
                    act.wait_ge(a_pT_ps, b + 1)
                    wait(act, a_out_ps, b - 1)
                    nc.scalar.copy(pTa[:, v, :, :], PS[:, 3, :].rearrange("p (t m) -> p t m", t=TPB)).then_inc(a_pT, 1)
                b = s - 1
                if has(b):
                    act.wait_ge(a_qk_ps, b + 1)
                    wait(act, a_sin, b)
                    nc.scalar.copy(qks[:, :], PS[:, 1, :]).then_inc(a_qks, 1)
                b = s - 2
                if has(b):
                    act.wait_ge(a_nb, b + 1)
                    wait(act, a_pT_ps, b - 1)
                    wait(act, a_rinv, b - 1)
                    for i in range(TPB):
                        last = nc.scalar.activation(pa[:, u, i, :], PS[:, 2, i * M:(i + 1) * M], ACT.Exp,
                                                    bias=nba[:, u, i:i + 1], scale=SCALE_A,
                                                    accum_out=rsa[:, u, i:i + 1])
                    last.then_inc(a_exp, 1)
                b = s - 1
                if has(b):
                    act.wait_ge(a_v_ps, b + 1)
                    wait(act, a_out_ps, b - 1)
                    nc.scalar.copy(va[:, v, :, :], PS[:, 5, 0:TPB * D].rearrange("p (t d) -> p t d", t=TPB)).then_inc(a_v, 1)

            def route(k):
                act.wait_ge(r_step, STEPS * k + SHIFT_STEP)
                nc.scalar.activation(r_ex[:, :, :], r_sh[:, :, :], ACT.Exp).then_inc(r_exp, 1)

            def experts(layer):
                n0 = NL * layer

                def ring(j):
                    return n0 if fixed(j) and j < 2 else n0 + (j - 1)

                def step(s, u):
                    w, v = u % 2, (u + 1) % 2
                    j = s - 2
                    if has(j, NL):
                        act.wait_ge(f_xT_ps, n0 + (j + 1))
                        wait(act, f_h_ps, ring(j))
                        nc.scalar.copy(xsT[:, w, :], PS[:, 2 + w, 0:P]).then_inc(f_xT, 1)
                    j = s - 3
                    if has(j, NL):
                        act.wait_ge(f_h_ps, n0 + (j + 1))
                        wait(act, f_y_ps, ring(j))
                        for c in range(FC):
                            last = nc.scalar.activation(hT[:, v, c, :], PS[:, v, c * P:(c + 1) * P], ACT.Gelu,
                                                        bias=w1b1[:, v, F + c:F + c + 1])
                        last.then_inc(f_gelu, 1)

                route(GROUPS * layer + 1)
                expert_steps(act, step, 0, first_quarter if layer == 0 else None)

            def first_quarter(i):
                attn_b(0, 0, 4 * i, 4 * i + 4)

            def qk_parts(q):
                act.wait_ge(b_qk_ps, q + 1)
                nc.scalar.copy(one_pass(QKh[:, 4 * q:4 * q + 4, :]),
                               PS[:, q % 2, :].rearrange("p (h d) -> p h d", h=4)).then_inc(b_qk, 1)

            def attn_b(s, u, h0=0, h1=H):
                hb, fb, v = s - 1, s - 2, (u + 1) % 2
                for h in range(h0, h1):
                    if h % 2 == 0:
                        b, hh = (hb, h - 5) if h >= 5 else (fb, h - 5 + H)
                        if has(b):
                            pair = hh // 2
                            act.wait_ge(b_av, b * H + (hh + 1))
                            if pair == 0:
                                wait(act, b_out_ps, b - 1)
                            nc.scalar.copy(yT[:, v if b is hb else u, pair, :],
                                                  PS[:, 7, 0:M]).then_inc(b_y, 1)
                    if has(hb):
                        cnt = hb * H + h
                        act.wait_ge(b_g_ps, cnt + 1)
                        wait(act, b_s_ps, cnt - 1)
                        nc.scalar.copy(one_pass(gh[:, h % 2, :]), PS[:, 4 + h % 2, P:M])
                        nc.scalar.copy(g0[:, h % 2, :], PS[:, 4 + h % 2, 0:P]).then_inc(b_g, 1)
                        if h < VT:
                            act.wait_ge(b_v_ps, hb * VT + (h + 1))
                            if h == 0:
                                wait(act, b_av, (hb - 1) * H)
                            to = (one_pass(vh[:, v, :]), v1[:, v, :])[h % 2]
                            nc.scalar.copy(to[:, h // 2 * VW:(h // 2 + 1) * VW], PS[:, 4 + h % 2, M:2 * M]
                                           ).then_inc(b_v, 1)
                    if h == 12 and has(s):
                        act.wait_ge(b_xT_ps, s + 1)
                        wait(act, b_s_ps, (s - 1) * H)
                        nc.scalar.copy(one_pass(xh[:, u, :]), PS[:, 4, M:2 * M])
                        nc.scalar.copy(xnT[:, u, :], PS[:, 4, M:2 * M]).then_inc(b_xT, 1)
                    b, hh = (hb, h - 3) if h >= 3 else (fb, h - 3 + H)
                    if has(b):
                        cnt = b * H + hh
                        act.wait_ge(b_pT_ps, cnt + 1)
                        wait(act, b_av, cnt - 1)
                        nc.scalar.copy(one_pass(pTh[:, hh % 2, :]), PS[:, 2 + hh % 2, 0:M]).then_inc(b_pTh, 1)
                    b, hh = (hb, h - 1) if h >= 1 else (fb, H - 1)
                    if has(b):
                        cnt = b * H + hh
                        act.wait_ge(b_nb, cnt + 1)
                        wait(act, b_pT_ps, cnt - 3)
                        wait(act, b_rinv, cnt - 3)
                        r = hh % 4
                        nc.scalar.activation(pb[:, r, 0:P], PS[:, hh % 2, 0:P], ACT.Exp, bias=nbb[:, r, 0:1],
                                             scale=-1.0, accum_out=rsb[:, r, 0:1])
                        nc.scalar.activation(pb[:, r, P:3 * P], PS[:, hh % 2, P:3 * P], ACT.Exp, bias=nbb[:, r, 1:2],
                                             scale=-1.0, accum_out=rsb[:, r, 1:2]).then_inc(b_exp, 1)
                    if h == 14 and has(fb):
                        router_copies(fb + NB, TPB * fb, u, 6)

            peeled(attn_a, 0, 8)
            turns(act, attn_a, 8, 14)
            route(0)
            turns(act, attn_a, 14, 16)
            for s in range(16, NB + 5):
                attn_a(s, s % 2)
                if s >= NB + 1:
                    qk_parts(s - (NB + 1))
            act.wait_ge(s_wb, 64)
            nc.scalar.copy(one_pass(WVBh[:, :]), WVB).then_inc(b_wv, 1)
            experts(0)
            act.wait_ge(lent_returned, 16 * LENT)
            peeled(attn_b, 1, 4)
            turns(act, attn_b, 4, 10)
            route(2)
            turns(act, attn_b, 10, 16)
            peeled(attn_b, 16, 18)
            experts(1)

        @block.vector
        def _(dve):
            dve.wait_ge(s_cst, 16)
            nc.vector.tensor_copy(upperb[:, :], CST[:, C_UP:C_UP + P])
            nc.vector.tensor_copy(onesb[:, :], CST[:, C_ONE:C_ONE + P])
            nc.vector.memset(half[:, :], -0.5).then_inc(s_castb, 1)

            def bn_stats(ln, n, tile, slot):
                dve.sem_inc(dve_waited)
                for i in range(TPB):
                    last = nc.vector.bn_stats(ln["stats"][:, slot, i, :], X[:, ds(tile + i), :])
                last.then_inc(ln["s_stats"], 1)

            def bn_aggr(ln, n, slot):
                dve.wait_ge(ln["s_stats"], n + 1)
                dve.sem_inc(dve_waited)
                for i in range(TPB):
                    last = nc.vector.bn_aggr(ln["mv"][:, slot, i, :], ln["stats"][:, slot, i, :])
                last.then_inc(ln["s_mv"], 1)

            def norm_var(ln, n, slot):
                dve.wait_ge(ln["s_mv"], n + 1)
                nc.vector.tensor_scalar(ln["var"][:, slot, :], ln["mv"][:, slot, :, 1], EPS, None,
                                        ALU.add).then_inc(ln["s_var"], 1)

            def norm_stats(ln, n, tile, slot):
                bn_stats(ln, n, tile, slot)
                bn_aggr(ln, n, slot)
                norm_var(ln, n, slot)

            def norm_apply(ln, n, tile, slot):
                dve.wait_ge(ln["s_rstd"], n + 1)
                for i in range(TPB):
                    last = nc.vector.tensor_scalar(ln["out"][:, slot, i, :], X[:, ds(tile + i), :],
                                                   ln["mv"][:, slot, i, 0:1], ln["rstd"][:, slot, i:i + 1],
                                                   ALU.subtract, ALU.mult)
                last.then_inc(ln["s_out"], 1)

            def logits(n, tile, bank):
                dve.wait_ge(r_lg_ps, n + 1)
                nc.vector.tensor_tensor(LG[:, ds(tile, TPB), :],
                                        PS[:, bank, M:M + TPB * E].rearrange("p (t e) -> p t e", t=TPB),
                                        BRS[:, None, :].to_broadcast([P, TPB, E]), ALU.add).then_inc(r_lg, 1)

            def attn_a(s, u):
                v = (u + 1) % 2
                if fixed(s) and s == 0:
                    dve.wait_ge(s_x0, 16)
                if fixed(s) and s == 2:
                    dve.wait_ge(s_x1, 16)
                b = s - 4
                if has(b):
                    dve.wait_ge(a_out_ps, b + 1)
                    dve.wait_ge(a_rinv, b + 1)
                    for i in range(TPB):
                        last = nc.vector.scalar_tensor_tensor(
                            out=X[:, ds(TPB * b + i), :], in0=PS[:, 6, i * D:(i + 1) * D], scalar=ria[:, u, i:i + 1],
                            in1=X[:, ds(TPB * b + i), :], op0=ALU.mult, op1=ALU.add)
                    last.then_inc(a_x, 1)
                if has(s):
                    if not fixed(s) or s >= 2:
                        dve.wait_ge(a_xT_ps, s - 1)
                    norm_stats(LN["A"], s, TPB * s, u)
                if has(b):
                    dve.wait_ge(a_x, b + 1)
                    wait(dve, r_tok, b - 1)
                    norm_stats(LN["F"], b, TPB * b, u)
                b = s - 3
                if has(b):
                    dve.wait_ge(a_exp, b + 1)
                    nc.vector.reciprocal(ria[:, v, :], rsa[:, v, :]).then_inc(a_rinv, 1)
                if has(s):
                    norm_apply(LN["A"], s, TPB * s, u)
                b = s - 4
                if has(b):
                    norm_apply(LN["F"], b, TPB * b, u)
                b = s - 1
                if has(b):
                    dve.wait_ge(a_qk_ps, b + 1)
                    if fixed(b) and b == 0:
                        dve.wait_ge(s_wa, 48)
                    wait(dve, a_rope, b)
                    nc.vector.tensor_tensor(rot[:, 0, :], PS[:, 0, :], ROPE[:, 0, :], ALU.mult).then_inc(a_rot, 1)
                b = s - 2
                if has(b):
                    dve.wait_ge(a_scores, b + 1)
                    wait(dve, a_exp, b - 1)
                    nc.vector.reduce_max(mxa[:, u, :], PS[:, 2, :].rearrange("p (t m) -> p t m", t=TPB),
                                         AX.X).then_inc(a_max, 1)
                    dve.wait_ge(a_max, b + 1)
                    nc.vector.tensor_scalar(nba[:, u, :], mxa[:, u, :], -SCALE_A, None, ALU.mult).then_inc(a_nb, 1)
                b = s - 1
                if has(b):
                    dve.wait_ge(a_rot, b + 1)
                    dve.wait_ge(a_sin, b + 1)
                    wait(dve, a_scores, b - 1)
                    nc.vector.tensor_tensor(qk[:, v, :, :].rearrange("p a m -> p (a m)"), rot[:, 0, :], rot[:, 1, :],
                                            ALU.add).then_inc(a_rope, 1)
                b = s - 5
                if has(b):
                    if fixed(b) and b == 0:
                        dve.wait_ge(s_wr, 32)
                    logits(b, TPB * b, 7)

            def route(k, between=None):
                g = k % GROUPS
                t0 = g * GT
                lg = LG[:, t0:t0 + GT, :]
                done = [STEPS * k]

                def then(ins):
                    done[0] += 1
                    ins.then_inc(r_step, 1)
                    if between is not None and done[0] % PACE == 0:
                        n = done[0] % STEPS // PACE
                        between((n if n else PACED) - 1)
                    dve.wait_ge(r_step, done[0])

                def over_e(ap):
                    return ap.unsqueeze(2).to_broadcast([P, GT, E])

                dve.wait_ge(r_lg, GB * (k + 1))
                then(nc.vector.reduce_max(r_mx[:, :], lg, AX.X))
                then(nc.vector.tensor_tensor(r_sh[:, :, :], lg, over_e(r_mx[:, :]), ALU.subtract))
                then(nc.vector.tensor_tensor(r_eq[:, :, :], lg, over_e(r_mx[:, :]), ALU.is_equal))
                e8 = CST[:, C_E8:C_E8 + E]
                then(nc.vector.tensor_tensor(r_eq[:, :, :], r_eq[:, :, :], e8[:, None, :].to_broadcast([P, GT, E]),
                                             ALU.mult))
                then(nc.vector.reduce_max(r_best[:, :], r_eq[:, :, :], AX.X))
                then(nc.vector.tensor_tensor(r_hot[:, :, :].rearrange("p e t -> p t e"),
                                             e8[:, None, :].to_broadcast([P, GT, E]), over_e(r_best[:, :]),
                                             ALU.is_equal))
                dve.wait_ge(r_exp, k + 1)
                then(nc.vector.reduce_sum(r_den[:, :], r_ex[:, :, :], AX.X))
                then(nc.vector.reciprocal(GATE[:, t0:t0 + GT], r_den[:, :]))
                dve.wait_ge(r_pre_ps, k + 1)
                then(nc.vector.tensor_copy(r_ps[:, :], PS[:, ROUTE_BANKS[k], 0:2 * E * GT]))
                assert done[0] == STEPS * k + READ_STEP
                pre = r_ps[:, 0:E * GT].rearrange("p (e t) -> p e t", e=E)
                tot = r_ps[:, E * GT:2 * E * GT]
                then(nc.vector.tensor_tensor_scan(r_inc[:, :, :].rearrange("p e t -> p (e t)"),
                                                  CST[:, C_SCAN:C_SCAN + E * GT], tot, 0.0, ALU.mult, ALU.add))
                then(nc.vector.tensor_tensor(r_exc[:, :, :].rearrange("p e t -> p (e t)"),
                                             r_inc[:, :, :].rearrange("p e t -> p (e t)"), tot, ALU.subtract))
                then(nc.vector.tensor_scalar(r_cnt[:, :], r_inc[:, :, GT - 1], float(P - 1), None, ALU.add))
                then(nc.vector.tensor_scalar(r_cnts[:, :], r_cnt[:, :], 7, None, ALU.logical_shift_right))
                then(nc.vector.tensor_copy(r_nt[:, :], r_cnts[:, :]))
                then(nc.vector.tensor_tensor_scan(r_cum[:, :], CST[:, C_ONE:C_ONE + E], r_nt[:, :], 0.0,
                                                  ALU.mult, ALU.add))
                then(nc.vector.tensor_tensor(r_base[:, :], r_cum[:, :], r_nt[:, :], ALU.subtract))
                then(nc.vector.scalar_tensor_tensor(
                    out=r_exc[:, :, :], in0=r_base[:, :].unsqueeze(2).to_broadcast([P, E, GT]), scalar=float(P),
                    in1=r_exc[:, :, :], op0=ALU.mult, op1=ALU.add))
                then(nc.vector.tensor_tensor(r_exc[:, :, :], pre, r_exc[:, :, :], ALU.add))
                then(nc.vector.tensor_tensor(r_exc[:, :, :], r_exc[:, :, :], r_hot[:, :, :], ALU.mult))
                then(nc.vector.reduce_sum(r_pos[:, :], r_exc[:, :, :].rearrange("p e t -> p t e"), AX.X))
                then(nc.vector.tensor_copy(r_posi[:, :], r_pos[:, :]))
                then(nc.vector.tensor_scalar(r_tile[:, :], r_posi[:, :], 7, None, ALU.logical_shift_right))
                then(nc.vector.tensor_copy(r_tilef[:, :], r_tile[:, :]))
                then(nc.vector.tensor_scalar(r_pos[:, :], r_pos[:, :], float(NJ), None, ALU.mult))
                then(nc.vector.scalar_tensor_tensor(out=POS[:, t0:t0 + GT], in0=r_tilef[:, :],
                                                    scalar=float(1 - NJ * P), in1=r_pos[:, :], op0=ALU.mult,
                                                    op1=ALU.add))
                then(nc.vector.tensor_tensor(
                    r_cmp[:, :, :], CST[:, C_TILE:C_TILE + NJ * E].rearrange("p (j e) -> p j e", e=E),
                    r_cum[:, None, :].to_broadcast([P, NJ, E]), ALU.is_ge))
                then(nc.vector.reduce_sum(r_te[:, :], r_cmp[:, :, :], AX.X))
                then(nc.vector.tensor_scalar(TE[:, g * NJ:(g + 1) * NJ], r_te[:, :], float(E - 1), None, ALU.min))
                assert done[0] == STEPS * (k + 1), done[0]

            def experts(layer):
                n0 = NL * layer

                def ring(j):
                    return n0 if fixed(j) and j < 2 else n0 + (j - 1)

                def step(s, u):
                    v, w, r = (u + 1) % 2, u % 2, u % RING
                    if has(s - 2, NL):
                        e = dve.value_load(TE[0:1, ds(s - 2)], min_val=0, max_val=E - 1)
                    j = s - 5
                    if has(j, NL):
                        n = n0 + j
                        dve.wait_ge(f_y_ps, n + 1)
                        nc.vector.tensor_tensor(XY[:, ds(j), 0:D], PS[:, 6 + v, 0:D],
                                                w2b2[:, (u - 5) % RING, FC * D:W2W], ALU.add).then_inc(f_y, 1)
                    j = s - 2
                    if has(j, NL):
                        n = n0 + j
                        if fixed(j) and j == 0 and layer == 0:
                            dve.wait_ge(s_w1, 32)
                            dve.wait_ge(s_w2, 16 * (FC + 1))
                            dve.wait_ge(b_qk_ps, 4)
                        wait(dve, f_h_ps, ring(j))
                        wait(dve, f_gelu, ring(j))
                        nc.vector.tensor_copy(w1b1[:, w, :], W1S[:, ds(e), :])
                        wait(dve, f_y, n0 if fixed(j) and j < RING else n0 + (j - (RING - 1)))
                        nc.vector.tensor_copy(w2b2[:, (u - 2) % RING, :], W2S[:, ds(e), :]).then_inc(f_w, 1)
                    j = s
                    if has(j, NL):
                        for kk in range(GROUPS):
                            for c, (j0, _) in enumerate(XCHUNKS):
                                if fixed(j) and j == (kk * NJ if kk else j0):
                                    dve.wait_ge(xs_in[GROUPS * layer + kk][c], 16)
                        wait(dve, f_xT_ps, ring(j))
                        nc.vector.tensor_copy(xs1[:, w, :], XY[:, ds(j), 0:D]).then_inc(f_in, 1)

                route(GROUPS * layer + 1, lambda i: step(i, i % RING))
                expert_steps(dve, step, PACED, first_quarter if layer == 0 else None)

            def first_quarter(i):
                attn_b(0, 0, 4 * i, 4 * i + 4)

            def qk_parts(q):
                dve.wait_ge(b_qk, q + 1)
                nc.vector.tensor_tensor(one_pass(QKl[:, 4 * q:4 * q + 4, :]),
                                        PS[:, q % 2, :].rearrange("p (h d) -> p h d", h=4),
                                        QKh[:, 4 * q:4 * q + 4, :], ALU.subtract).then_inc(b_qkl, 1)

            def combine(tile, s_inc):
                for i in range(TPB):
                    last = nc.vector.scalar_tensor_tensor(
                        out=X[:, ds(tile + i), :], in0=TOK[:, ds(tile + i), 0:D], scalar=GATE[:, ds(tile + i)],
                        in1=X[:, ds(tile + i), :], op0=ALU.mult, op1=ALU.add)
                if s_inc is not None:
                    last.then_inc(s_inc, 1)

            def attn_b(s, u, h0=0, h1=H):
                hb, fb, v = s - 1, s - 2, (u + 1) % 2
                for h in range(h0, h1):
                    b, hh = (hb, h - 2) if h >= 2 else (fb, h - 2 + H)
                    if has(b):
                        cnt = b * H + hh
                        dve.wait_ge(b_exp, cnt + 1)
                        wait(dve, b_p, cnt - 3)
                        nc.vector.reciprocal(rib[:, hh % 4, :], rsb[:, hh % 4, :]).then_inc(b_rinv, 1)
                    b, hh = (hb, h - 1) if h >= 1 else (fb, H - 1)
                    if has(b):
                        cnt = b * H + hh
                        dve.wait_ge(b_s_ps, cnt + 1)
                        dve.sem_inc(dve_waited)
                        for c0, c1, m in ((0, P, C_MASK), (P, 3 * P, C_ZERO)):
                            ps = PS[:, hh % 2, c0:c1]
                            last = nc.vector.tensor_tensor_reduce(
                                ps, ps, CST[:, m:m + c1 - c0], -SCALE_B, HIGHEST, ALU.add, ALU.min,
                                nbb[:, hh % 4, c0 // P:c0 // P + 1])
                        last.then_inc(b_nb, 1)
                    if has(hb):
                        dve.wait_ge(b_g, hb * H + (h + 1))
                        if h < VT:
                            dve.wait_ge(b_v, hb * VT + (h + 1))
                        if h == 12 and has(s):
                            dve.wait_ge(b_xT, s + 1)
                        nc.vector.tensor_tensor(one_pass(gl[:, h % 2, :]), PS[:, 4 + h % 2, P:M], gh[:, h % 2, :],
                                                ALU.subtract).then_inc(b_gl, 1)
                    b, hh = (hb, h - 3) if h >= 3 else (fb, h - 3 + H)
                    if has(b):
                        cnt = b * H + hh
                        dve.wait_ge(b_pTh, cnt + 1)
                        nc.vector.tensor_tensor(one_pass(pTl[:, hh % 2, :]), PS[:, 2 + hh % 2, 0:M], pTh[:, hh % 2, :],
                                                ALU.subtract)
                        nc.vector.tensor_copy(pT1[:, hh % 2, :], PS[:, 2 + hh % 2, M:3 * P]).then_inc(b_pT, 1)
                    if h < VT and h % 2 == 0 and has(hb):
                        dve.wait_ge(b_v, hb * VT + (h + 1))
                        c = slice(h // 2 * VW, (h // 2 + 1) * VW)
                        nc.vector.tensor_tensor(one_pass(vl[:, v, c]), PS[:, 4, M:2 * M], vh[:, v, c],
                                                ALU.subtract).then_inc(b_vl, 1)
                    if h == 9 and has(fb):
                        dve.wait_ge(b_out_ps, fb + 1)
                        nc.vector.tensor_tensor(X[:, ds(TPB * fb, TPB), :],
                                                PS[:, 6, 0:TPB * D].rearrange("p (t d) -> p t d", t=TPB),
                                                X[:, ds(TPB * fb, TPB), :], ALU.add).then_inc(b_x, 1)
                    if h == 10 and has(fb):
                        dve.wait_ge(b_x, fb + 1)
                        dve.wait_ge(r_tok, fb + (NB - 1))
                        bn_stats(LN["F"], fb + NB, TPB * fb, u)
                    if h == 11 and has(fb):
                        bn_aggr(LN["F"], fb + NB, u)
                    if h == 12 and has(fb):
                        norm_var(LN["F"], fb + NB, u)
                    if h == 13 and has(fb):
                        norm_apply(LN["F"], fb + NB, TPB * fb, u)
                    if h == 15 and has(fb):
                        logits(fb + NB, TPB * fb, 6)
                    if h == 3 and has(s):
                        if fixed(s) and s in (0, GB):
                            dve.wait_ge(gathered[s // GB], 16)
                        combine(TPB * s, b_comb)
                    if h == 4 and has(s):
                        dve.wait_ge(b_comb, s + 1)
                        wait(dve, b_xT_ps, s - 1)
                        bn_stats(LN["B"], s, TPB * s, u)
                    if h == 5 and has(s):
                        bn_aggr(LN["B"], s, u)
                    if h == 6 and has(s):
                        norm_var(LN["B"], s, u)
                    if h == 8 and has(s):
                        norm_apply(LN["B"], s, TPB * s, u)
                    if h == 12 and has(s):
                        dve.wait_ge(b_xT, s + 1)
                        nc.vector.tensor_tensor(one_pass(xl[:, u, :]), PS[:, 4, M:2 * M], xh[:, u, :],
                                                ALU.subtract).then_inc(b_xl, 1)

            peeled(attn_a, 0, 8)
            turns(dve, attn_a, 8, 14)
            route(0)
            turns(dve, attn_a, 14, 16)
            for s in range(16, NB + 5):
                attn_a(s, s % 2)
                if s >= NB + 1:
                    qk_parts(s - (NB + 1))
            experts(0)
            dve.wait_ge(b_wv, 1)
            nc.vector.tensor_tensor(one_pass(WVBl[:, :]), WVB, WVBh[:, :], ALU.subtract).then_inc(b_qkl, 1)
            dve.wait_ge(lent_returned, 16 * LENT)
            peeled(attn_b, 1, 4)
            turns(dve, attn_b, 4, 8)
            peeled(attn_b, 8, 10)
            route(2)
            turns(dve, attn_b, 10, 16)
            peeled(attn_b, 16, 18)
            experts(1)
            dve.wait_ge(gathered[2], 16)
            for q in range(8):
                if q >= 4:
                    dve.wait_ge(last_gathered[q - 4], 16)
                for b in range(2):
                    combine(4 * q + TPB * b, x_done if b == 1 else None)

        @block.tensor
        def _(pe):
            mm, tr = nc.tensor.matmul, nc.tensor.transpose

            def split(ps, lhs, rhs):
                mm(ps, one_pass(lhs[0]), one_pass(rhs[0]), start=True, stop=False)
                mm(ps, one_pass(lhs[0]), one_pass(rhs[1]), start=False, stop=False)
                return mm(ps, one_pass(lhs[1]), one_pass(rhs[0]), start=False, stop=True)

            def router_T(n, slot, bank):
                pe.wait_ge(LN["F"]["s_out"], n + 1)
                for i in range(TPB):
                    last = tr(PS[:, bank, i * P:(i + 1) * P], LN["F"]["out"][:, slot, i, :], ident)
                last.then_inc(r_xT_ps, 1)

            def router(n, slot, bank):
                pe.wait_ge(r_xT, n + 1)
                for i in range(TPB):
                    last = mm(PS[:, bank, M + i * E:M + (i + 1) * E], fT[:, slot, i * P:(i + 1) * P], WRS[:, :],
                              start=True, stop=True)
                last.then_inc(r_lg_ps, 1)

            def attn_a(s, u):
                v = (u + 1) % 2
                b = s - 1
                if has(b):
                    pe.wait_ge(LN["A"]["s_out"], b + 1)
                    wait(pe, a_xT, b)
                    for i in range(TPB):
                        last = tr(PS[:, 4, i * P:(i + 1) * P], LN["A"]["out"][:, v, i, :], ident)
                    last.then_inc(a_xT_ps, 1)
                b = s - 5
                if has(b):
                    if fixed(b) and b == 0:
                        pe.wait_ge(s_wr, 32)
                    wait(pe, r_lg, b)
                    router_T(b, v, 7)
                b = s - 3
                if has(b):
                    pe.wait_ge(a_exp, b + 1)
                    wait(pe, a_pT, b)
                    for kc in range(TPB):
                        for i in range(TPB):
                            last = tr(PS[:, 3, kc * M + i * P:kc * M + (i + 1) * P],
                                      pa[:, v, i, kc * P:(kc + 1) * P], ident)
                    last.then_inc(a_pT_ps, 1)
                b = s - 1
                if has(b):
                    if fixed(b) and b == 0:
                        pe.wait_ge(s_wa, 48)
                    pe.wait_ge(a_xT, b + 1)
                    wait(pe, a_rot, b)
                    wait(pe, a_qks, b)
                    for i in range(2):
                        for w in range(2):
                            last = mm(PS[:, i, w * M:(w + 1) * M], WQK[:, 2 * w + i, :], xnT[:, v, :],
                                      start=True, stop=True)
                    last.then_inc(a_qk_ps, 1)
                b = s - 2
                if has(b):
                    pe.wait_ge(a_rope, b + 1)
                    wait(pe, a_exp, b)
                    for i in range(TPB):
                        last = mm(PS[:, 2, i * M:(i + 1) * M], qk[:, u, 0, i * P:(i + 1) * P], qk[:, u, 1, :],
                                  start=True, stop=True)
                    last.then_inc(a_scores, 1)
                b = s - 1
                if has(b):
                    wait(pe, a_v, b)
                    for i in range(TPB):
                        last = mm(PS[:, 5, i * D:(i + 1) * D], xnT[:, v, i * P:(i + 1) * P], WVA[:, :],
                                  start=True, stop=True)
                    last.then_inc(a_v_ps, 1)
                b = s - 3
                if has(b):
                    pe.wait_ge(a_pT, b + 1)
                    pe.wait_ge(a_v, b + 1)
                    wait(pe, a_x, b)
                    for i in range(TPB):
                        for kc in range(TPB):
                            last = mm(PS[:, 6, i * D:(i + 1) * D], pTa[:, v, kc, i * P:(i + 1) * P],
                                      va[:, v, kc, :], start=kc == 0, stop=kc == TPB - 1)
                    last.then_inc(a_out_ps, 1)
                b = s - 5
                if has(b):
                    router(b, v, 7)

            def route(k):
                bank = ROUTE_BANKS[k]
                pe.wait_ge(r_step, STEPS * k + HOT_STEP)
                if k == 2:
                    pe.wait_ge(r_lg, GB * (k + 1))
                hot = r_hot[:, :, :].rearrange("p e t -> p (e t)")
                mm(PS[:, bank, 0:E * GT], upperb[:, :], hot, start=True, stop=True)
                mm(PS[:, bank, E * GT:2 * E * GT], onesb[:, :], hot, start=True, stop=True).then_inc(r_pre_ps, 1)
                if k % GROUPS == 0:
                    pe.wait_ge(r_step, STEPS * k + READ_STEP)

            def experts(layer):
                n0 = NL * layer

                def ring(j):
                    return n0 if fixed(j) and j < 2 else n0 + (j - 1)

                def step(s, u):
                    v, w, r = (u + 1) % 2, u % 2, u % RING
                    j = s - 1
                    if has(j, NL):
                        n = n0 + j
                        pe.wait_ge(f_in, n + 1)
                        wait(pe, f_xT, ring(j))
                        tr(PS[:, 2 + v, 0:P], xs1[:, v, :], ident).then_inc(f_xT_ps, 1)
                    j = s - 3
                    if has(j, NL):
                        n = n0 + j
                        pe.wait_ge(f_xT, n + 1)
                        pe.wait_ge(f_w, n + 1)
                        wait(pe, f_gelu, ring(j))
                        for c in range(FC):
                            last = mm(PS[:, v, c * P:(c + 1) * P], w1b1[:, v, c * P:(c + 1) * P], xsT[:, v, :],
                                      start=True, stop=True)
                        last.then_inc(f_h_ps, 1)
                    j = s - 4
                    if has(j, NL):
                        n = n0 + j
                        pe.wait_ge(f_gelu, n + 1)
                        wait(pe, f_y, ring(j))
                        for c in range(FC):
                            last = mm(PS[:, 6 + w, 0:D], hT[:, w, c, :], w2b2[:, r, c * D:(c + 1) * D],
                                      start=c == 0, stop=c == FC - 1)
                        last.then_inc(f_y_ps, 1)

                route(GROUPS * layer + 1)
                expert_steps(pe, step, 0, first_quarter if layer == 0 else None)

            def first_quarter(i):
                attn_b(0, 0, 4 * i, 4 * i + 4)

            def qk_parts(q):
                if q == 0:
                    pe.wait_ge(s_wb, 64)
                    pe.wait_ge(a_rope, NB)
                elif q >= 2:
                    pe.wait_ge(b_qkl, q - 1)
                for h in range(4 * q, 4 * q + 4):
                    last = mm(PS[:, q % 2, (h % 4) * P:(h % 4 + 1) * P], WQB[:, h, :], WKB[:, h, :],
                              start=True, stop=True)
                last.then_inc(b_qk_ps, 1)

            def attn_b(s, u, h0=0, h1=H):
                hb, fb, v = s - 1, s - 2, (u + 1) % 2

                def scores(b, hh, slot):
                    cnt = b * H + hh
                    pe.wait_ge(b_g, cnt + 1)
                    pe.wait_ge(b_gl, cnt + 1)
                    wait(pe, b_exp, cnt - 1)
                    ps = PS[:, hh % 2, :]
                    mm(ps[:, 0:P], g0[:, hh % 2, :], xnT[:, slot, 0:P], start=True, stop=True)
                    split(ps[:, P:3 * P], (gh[:, hh % 2, :], gl[:, hh % 2, :]), (xh[:, slot, :], xl[:, slot, :])
                          ).then_inc(b_s_ps, 1)

                def transposes(b, hh):
                    cnt = b * H + hh
                    pe.wait_ge(b_p, cnt + 1)
                    wait(pe, b_pT, cnt - 1)
                    for c in range(3):
                        last = tr(PS[:, 2 + hh % 2, c * P:(c + 1) * P], pb[:, hh % 4, c * P:(c + 1) * P], ident)
                    last.then_inc(b_pT_ps, 1)

                def product(b, hh, slot):
                    cnt = b * H + hh
                    pe.wait_ge(b_pT, cnt + 1)
                    if hh % 4 == 0:
                        pe.wait_ge(b_v, b * VT + (hh // 2 + 2))
                        pe.wait_ge(b_vl, b * (VT // 2) + (hh // 4 + 1))
                    if hh % 2 == 0:
                        wait(pe, b_y, b * NPAIR + hh // 2)
                    head = head_at(hh)
                    q = DK * (head % 2)
                    c = slice((head - 1) * DK if q else head * DK, (head + 1) * DK)
                    split(PS[0:q + DK, 7, 0:M], (vh[:, slot, c], vl[:, slot, c]), (pTh[:, hh % 2, :], pTl[:, hh % 2, :]))
                    c = slice(head * DK, (head + 1) * DK)
                    last = mm(PS[q:q + DK, 7, P:M], v1[:, slot, c], pT1[:, hh % 2, :],
                              start=False, stop=True, skip_group_check=True)
                    last.then_inc(b_av, 1)

                for h in range(h0, h1):
                    if has(hb):
                        cnt = hb * H + h
                        if h == 0:
                            pe.wait_ge(b_xT, hb + 1)
                            pe.wait_ge(b_xl, hb + 1)
                        wait(pe, b_g, cnt - 1)
                        wait(pe, b_gl, cnt - 1)
                        if 2 <= h < VT + 2:
                            pe.wait_ge(b_v, hb * VT + (h - 1))
                            if h % 2 == 0:
                                pe.wait_ge(b_vl, hb * (VT // 2) + h // 2)
                        if h == 14 and has(s):
                            pe.wait_ge(b_xT, s + 1)
                            pe.wait_ge(b_xl, s + 1)
                        if h < VT:
                            i, c = h % 2, slice(h // 2 * VW, (h // 2 + 1) * VW)
                            split(PS[:, 4 + i, M:2 * M], [x_[:, v, i * P:(i + 1) * P] for x_ in (xh, xl)],
                                  [w_[:, c] for w_ in (WVBh, WVBl)]).then_inc(b_v_ps, 1)
                    if h == 12 and has(s):
                        pe.wait_ge(LN["B"]["s_out"], s + 1)
                        for i in range(TPB):
                            last = tr(PS[:, 4, M + i * P:M + (i + 1) * P], LN["B"]["out"][:, u, i, :], ident)
                        last.then_inc(b_xT_ps, 1)
                    if has(hb):
                        split(PS[:, 4 + h % 2, 0:M], (QKh[:, head_at(h), :], QKl[:, head_at(h), :]),
                              (xh[:, v, :], xl[:, v, :])).then_inc(b_g_ps, 1)
                    if h >= 1 and has(hb):
                        scores(hb, h - 1, v)
                    if h == 0 and has(fb):
                        scores(fb, H - 1, u)
                    if h >= 3 and has(hb):
                        transposes(hb, h - 3)
                    if h < 3 and has(fb):
                        transposes(fb, h - 3 + H)
                    if h >= 4 and has(hb):
                        product(hb, h - 4, v)
                    if h < 4 and has(fb):
                        product(fb, h - 4 + H, u)
                    if 5 <= h < 9 and has(fb):
                        i = (h - 5) // 2
                        if h == 5:
                            pe.wait_ge(b_y, fb * NPAIR + NPAIR)
                            if has(s - 3):
                                pe.wait_ge(r_lg, s + (NB - 2))
                        for k in range(NPAIR // 2):
                            pair = (h - 5) % 2 * (NPAIR // 2) + k
                            last = mm(PS[:, 6, i * D:(i + 1) * D], yT[:, u, pair, i * P:(i + 1) * P], WO[:, pair, :],
                                      start=pair == 0, stop=pair == NPAIR - 1)
                        if h == 8:
                            last.then_inc(b_out_ps, 1)
                    if h == 14 and has(fb):
                        router_T(fb + NB, u, 6)
                    if h == 15 and has(fb):
                        router(fb + NB, u, 6)

            pe.wait_ge(s_cst, 16)
            pe.wait_ge(s_castb, 1)
            peeled(attn_a, 0, 8)
            turns(pe, attn_a, 8, 14)
            route(0)
            turns(pe, attn_a, 14, 16)
            for s in range(16, NB + 5):
                attn_a(s, s % 2)
                if s >= NB + 1:
                    qk_parts(s - (NB + 1))
            pe.wait_ge(b_qkl, 4)
            experts(0)
            pe.wait_ge(f_y, 2 * NJ)
            pe.wait_ge(b_qkl, 5)
            peeled(attn_b, 1, 4)
            turns(pe, attn_b, 4, 10)
            route(2)
            turns(pe, attn_b, 10, 16)
            peeled(attn_b, 16, 18)
            experts(1)


STEPS, SHIFT_STEP, HOT_STEP, READ_STEP = 28, 2, 6, 9
ROUTE_BANKS = (7, 5, 6, 5)
PACE = 4
PACED = STEPS // PACE

_OUT = (NB, M, D)


def tables():
    i = np.arange(D // 2, dtype=np.float32)
    theta = np.power(np.float32(10000.0), (np.float32(-2.0) * (i - np.float32(1.0)) / np.float32(D)).astype(np.float32))
    ang = (np.arange(M, dtype=np.float32)[:, None] * theta[None, :].astype(np.float32)).astype(np.float32)
    cos, sin = np.cos(ang).T, np.sin(ang).T
    rope = np.zeros((P, 2, 2, M), np.float32)
    rope[0::2, 0], rope[1::2, 0] = cos[:, None, :], cos[:, None, :]
    rope[0::2, 1], rope[1::2, 1] = sin[:, None, :], -sin[:, None, :]
    cst = np.zeros((P, C_W), np.float32)
    r = np.arange(P)
    cst[:, C_ID:C_ID + P] = np.eye(P)
    cst[:, C_UP:C_UP + P] = r[:, None] < r[None, :]
    cst[:, C_ONE:C_ONE + P] = 1.0
    cst[:, C_ZERO:C_ZERO + P] = 0.0
    cst[:, C_MASK:C_MASK + P] = np.where(r[:, None] < r[None, :], MASKED, 0.0)
    cst[:, C_E8:C_E8 + E] = E - np.arange(E)
    cst[:, C_SCAN:C_SCAN + E * GT] = (np.arange(E * GT) % GT != 0)
    cst[:, C_TILE:C_TILE + NJ * E] = np.arange(NJ * E) // E
    return rope.reshape(P, 2, 2 * M), cst


def kernel(**inputs):
    import concourse.bacc as _bacc
    from concourse.bass_utils import run_bass_kernel_spmd as _run

    a = {n.replace("L0_", ""): np.asarray(v) for n, v in inputs.items()}
    swap = np.arange(D) ^ 1
    wq, wk = a["attn_a_wq"].T, a["attn_a_wk"].T
    rope, cst = tables()
    ids = np.concatenate([np.arange(NT)[None, :] % GT * P + np.arange(P)[:, None],
                          NONE + np.arange(P * NJ).reshape(P, NJ)], axis=1).astype(np.int32)
    arrays = {
        "ids": ids,
        "x": a["attn_a_x"],
        "wqk_a": np.stack([wq, wq[:, swap], wk, wk[:, swap]], axis=1),
        "wv_a": a["attn_a_wv"].T,
        "rope": rope,
        "w_q": a["attn_b_w_q"],
        "w_k": a["attn_b_w_k"],
        "wv_b": a["attn_b_w_v"].reshape(H * DK, D).T,
        "w_o": a["attn_b_w_o"],
        "W1": a["ffn_W1"],
        "b1t": a["ffn_b1"].reshape(E, FC, P).transpose(2, 0, 1),
        "W2": a["ffn_W2"],
        "b2": a["ffn_b2"],
        "Wr": a["ffn_Wr"],
        "br": a["ffn_br"],
        "cst": cst,
    }
    arrays = {f"in_{n}": np.ascontiguousarray(v) for n, v in arrays.items()}
    nc = _bacc.Bacc("TRN2", target_bir_lowering=False, num_devices=1)
    args = [nc.dram_tensor(n, v.shape, mybir.dt.from_np(v.dtype), kind="ExternalInput").ap()
            for n, v in arrays.items()]
    out = nc.dram_tensor("out_dram", _OUT, F32, kind="ExternalOutput").ap()
    build(nc, *args, out)
    r = _run(nc, [arrays], core_ids=[0])
    return r.results[0]["out_dram"]
```
